# Optimizing a Trainium2 kernel written in Bass

```python
import numpy as np
import jax
import jax.numpy as jnp

def _softmax(x, axis=-1):
    return jax.nn.softmax(x, axis=axis)

def _gelu(x):
    return jax.nn.gelu(x, approximate=True)

def _silu(x):
    return jax.nn.silu(x)

def _sigmoid(x):
    return jax.nn.sigmoid(x)

def _layernorm(x, axis=-1, eps=1e-05):
    m = jnp.mean(x, axis=axis, keepdims=True)
    v = jnp.var(x, axis=axis, keepdims=True)
    return (x - m) / jnp.sqrt(v + eps)

def _scatter_add(tgt, idx, src, axis=0):
    return tgt.at[idx].add(src)

def _segment_sum(src, seg, n):
    return jax.ops.segment_sum(src, seg, n)
kernel_name = 'mk_sandwich_d1_jaxref_r4_4530ab'

def setup_inputs(seed: int=0):
    np.random.seed(seed)
    _w = jnp.asarray

    def _L0_attn_setup():
        import jax, jax.numpy as jnp
        import numpy as np
        from jax import lax
        B, L, D = (2, 256, 256)
        N_LAYER, D_STATE, D_CONV = (4, 16, 4)
        E = 2 * D
        DT_RANK = (D + 15) // 16
        EPS = 1e-05

        def rmsnorm(x, w):
            v = jnp.mean(jnp.square(x), axis=-1, keepdims=True)
            return x * lax.rsqrt(v + EPS) * w

        def mamba_mixer(x, ipw, cw, cb, xpw, dtw, dtb, A_log, Dp, opw):
            xz = jnp.einsum('bld,ed->ble', x, ipw)
            xi, z = jnp.split(xz, 2, axis=-1)
            xt = jnp.moveaxis(xi, 1, 2)
            xc = lax.conv_general_dilated(xt, cw[:, None, :], (1,), [(D_CONV - 1, 0)], feature_group_count=E, dimension_numbers=('NCH', 'OIH', 'NCH'))
            xc = jax.nn.silu(xc + cb[None, :, None])
            u = jnp.moveaxis(xc, 1, 2)
            xdb = jnp.einsum('ble,re->blr', u, xpw)
            dt_in, Bm, C = jnp.split(xdb, [DT_RANK, DT_RANK + D_STATE], axis=-1)
            dt = jax.nn.softplus(jnp.einsum('blr,er->ble', dt_in, dtw) + dtb)
            A = -jnp.exp(A_log)

            def step(h, inp):
                dt_t, B_t, C_t, u_t = inp
                dA = jnp.exp(dt_t[..., None] * A)
                h = dA * h + (dt_t * u_t)[..., None] * B_t[:, None, :]
                return (h, jnp.einsum('ben,bn->be', h, C_t))
            h0 = jnp.zeros((x.shape[0], E, D_STATE), x.dtype)
            xs = (jnp.moveaxis(dt, 1, 0), jnp.moveaxis(Bm, 1, 0), jnp.moveaxis(C, 1, 0), jnp.moveaxis(u, 1, 0))
            _, ys = lax.scan(step, h0, xs)
            y = jnp.moveaxis(ys, 0, 1) + u * Dp
            y = y * jax.nn.silu(z)
            return jnp.einsum('ble,de->bld', y, opw)
        key = jax.random.key(seed)
        ks = jax.random.split(key, 8)
        s = 0.02
        A_log = jnp.broadcast_to(jnp.log(jnp.arange(1, D_STATE + 1, dtype=jnp.float32)), (N_LAYER, E, D_STATE)) + 0.0
        return {'hidden_states': jax.random.normal(ks[0], (B, L, D), jnp.float32), 'in_proj_w': jax.random.normal(ks[1], (N_LAYER, 2 * E, D), jnp.float32) * s, 'conv_w': jax.random.normal(ks[2], (N_LAYER, E, D_CONV), jnp.float32) * 0.2, 'conv_b': jnp.zeros((N_LAYER, E), jnp.float32), 'x_proj_w': jax.random.normal(ks[3], (N_LAYER, DT_RANK + 2 * D_STATE, E), jnp.float32) * s, 'dt_proj_w': jax.random.normal(ks[4], (N_LAYER, E, DT_RANK), jnp.float32) * 0.1, 'dt_proj_b': jnp.full((N_LAYER, E), -4.6, jnp.float32), 'A_log': A_log, 'D_param': jnp.ones((N_LAYER, E), jnp.float32), 'out_proj_w': jax.random.normal(ks[5], (N_LAYER, D, E), jnp.float32) * s, 'norm_w': jnp.ones((N_LAYER, D), jnp.float32), 'norm_f_w': jnp.ones((D,), jnp.float32)}
    _L0_attn_in = _L0_attn_setup()

    def _L0_ffn_setup():
        import jax, jax.numpy as jnp
        import numpy as np
        D_IN, D_HID = (256, 1024)

        def _ternary(key, shape):
            return jax.random.randint(key, shape, -1, 2).astype(jnp.float32)

        def _tlin(x, w, s):
            return jnp.einsum('bsi,oi->bso', x, w) * s
        key = jax.random.key(seed)
        ks = jax.random.split(key, 12)
        inv = lambda fan: 1.0 / np.sqrt(fan).astype(np.float32)
        return {'x': jax.random.normal(ks[0], (4, 512, D_IN), dtype=jnp.float32), 'w1_w': _ternary(ks[1], (D_HID, D_IN)), 'w1_s': jax.random.uniform(ks[2], (D_HID,), dtype=jnp.float32) * inv(D_IN), 'w2_w': _ternary(ks[3], (D_HID, D_IN)), 'w2_s': jax.random.uniform(ks[4], (D_HID,), dtype=jnp.float32) * inv(D_IN), 'h1_w': _ternary(ks[5], (D_HID, D_HID)), 'h1_s': jax.random.uniform(ks[6], (D_HID,), dtype=jnp.float32) * inv(D_HID), 'h2_w': _ternary(ks[7], (D_HID, D_HID)), 'h2_s': jax.random.uniform(ks[8], (D_HID,), dtype=jnp.float32) * inv(D_HID), 'w3_w': _ternary(ks[9], (D_IN, D_HID)), 'w3_s': jax.random.uniform(ks[10], (D_IN,), dtype=jnp.float32) * inv(D_HID)}
    _L0_ffn_in = _L0_ffn_setup()
    _d = {'L0_attn_hidden_states': _L0_attn_in['hidden_states'], 'L0_attn_in_proj_w': _L0_attn_in['in_proj_w'], 'L0_attn_conv_w': _L0_attn_in['conv_w'], 'L0_attn_conv_b': _L0_attn_in['conv_b'], 'L0_attn_x_proj_w': _L0_attn_in['x_proj_w'], 'L0_attn_dt_proj_w': _L0_attn_in['dt_proj_w'], 'L0_attn_dt_proj_b': _L0_attn_in['dt_proj_b'], 'L0_attn_A_log': _L0_attn_in['A_log'], 'L0_attn_D_param': _L0_attn_in['D_param'], 'L0_attn_out_proj_w': _L0_attn_in['out_proj_w'], 'L0_attn_norm_w': _L0_attn_in['norm_w'], 'L0_attn_norm_f_w': _L0_attn_in['norm_f_w'], 'L0_ffn_w1_w': _L0_ffn_in['w1_w'], 'L0_ffn_w1_s': _L0_ffn_in['w1_s'], 'L0_ffn_w2_w': _L0_ffn_in['w2_w'], 'L0_ffn_w2_s': _L0_ffn_in['w2_s'], 'L0_ffn_h1_w': _L0_ffn_in['h1_w'], 'L0_ffn_h1_s': _L0_ffn_in['h1_s'], 'L0_ffn_h2_w': _L0_ffn_in['h2_w'], 'L0_ffn_h2_s': _L0_ffn_in['h2_s'], 'L0_ffn_w3_w': _L0_ffn_in['w3_w'], 'L0_ffn_w3_s': _L0_ffn_in['w3_s']}
    _x0 = _d['L0_attn_hidden_states']
    _d['L0_attn_hidden_states'] = jax.random.normal(jax.random.fold_in(jax.random.key(seed), 1), (4, 1024, 256), dtype=_x0.dtype)
    del _x0
    return _d

def reference(L0_attn_hidden_states, L0_attn_in_proj_w, L0_attn_conv_w, L0_attn_conv_b, L0_attn_x_proj_w, L0_attn_dt_proj_w, L0_attn_dt_proj_b, L0_attn_A_log, L0_attn_D_param, L0_attn_out_proj_w, L0_attn_norm_w, L0_attn_norm_f_w, L0_ffn_w1_w, L0_ffn_w1_s, L0_ffn_w2_w, L0_ffn_w2_s, L0_ffn_h1_w, L0_ffn_h1_s, L0_ffn_h2_w, L0_ffn_h2_s, L0_ffn_w3_w, L0_ffn_w3_s):

    def _L0_attn_ref(hidden_states, in_proj_w, conv_w, conv_b, x_proj_w, dt_proj_w, dt_proj_b, A_log, D_param, out_proj_w, norm_w, norm_f_w):
        import jax, jax.numpy as jnp
        import numpy as np
        from jax import lax
        B, L, D = (2, 256, 256)
        N_LAYER, D_STATE, D_CONV = (4, 16, 4)
        E = 2 * D
        DT_RANK = (D + 15) // 16
        EPS = 1e-05

        def rmsnorm(x, w):
            v = jnp.mean(jnp.square(x), axis=-1, keepdims=True)
            return x * lax.rsqrt(v + EPS) * w

        def mamba_mixer(x, ipw, cw, cb, xpw, dtw, dtb, A_log, Dp, opw):
            xz = jnp.einsum('bld,ed->ble', x, ipw)
            xi, z = jnp.split(xz, 2, axis=-1)
            xt = jnp.moveaxis(xi, 1, 2)
            xc = lax.conv_general_dilated(xt, cw[:, None, :], (1,), [(D_CONV - 1, 0)], feature_group_count=E, dimension_numbers=('NCH', 'OIH', 'NCH'))
            xc = jax.nn.silu(xc + cb[None, :, None])
            u = jnp.moveaxis(xc, 1, 2)
            xdb = jnp.einsum('ble,re->blr', u, xpw)
            dt_in, Bm, C = jnp.split(xdb, [DT_RANK, DT_RANK + D_STATE], axis=-1)
            dt = jax.nn.softplus(jnp.einsum('blr,er->ble', dt_in, dtw) + dtb)
            A = -jnp.exp(A_log)

            def step(h, inp):
                dt_t, B_t, C_t, u_t = inp
                dA = jnp.exp(dt_t[..., None] * A)
                h = dA * h + (dt_t * u_t)[..., None] * B_t[:, None, :]
                return (h, jnp.einsum('ben,bn->be', h, C_t))
            h0 = jnp.zeros((x.shape[0], E, D_STATE), x.dtype)
            xs = (jnp.moveaxis(dt, 1, 0), jnp.moveaxis(Bm, 1, 0), jnp.moveaxis(C, 1, 0), jnp.moveaxis(u, 1, 0))
            _, ys = lax.scan(step, h0, xs)
            y = jnp.moveaxis(ys, 0, 1) + u * Dp
            y = y * jax.nn.silu(z)
            return jnp.einsum('ble,de->bld', y, opw)
        h, residual = (hidden_states, None)
        for i in range(N_LAYER):
            residual = h if residual is None else h + residual
            hn = rmsnorm(residual, norm_w[i])
            h = mamba_mixer(hn, in_proj_w[i], conv_w[i], conv_b[i], x_proj_w[i], dt_proj_w[i], dt_proj_b[i], A_log[i], D_param[i], out_proj_w[i])
        return rmsnorm(h + residual, norm_f_w)

    def _L0_ffn_ref(x, w1_w, w1_s, w2_w, w2_s, h1_w, h1_s, h2_w, h2_s, w3_w, w3_s):
        import jax, jax.numpy as jnp
        import numpy as np
        D_IN, D_HID = (256, 1024)

        def _ternary(key, shape):
            return jax.random.randint(key, shape, -1, 2).astype(jnp.float32)

        def _tlin(x, w, s):
            return jnp.einsum('bsi,oi->bso', x, w) * s
        h = jax.nn.silu(_tlin(x, w1_w, w1_s)) * _tlin(x, w2_w, w2_s)
        h = jax.nn.gelu(_tlin(h, h1_w, h1_s), approximate=False)
        h = jax.nn.gelu(_tlin(h, h2_w, h2_s), approximate=False)
        return _tlin(h, w3_w, w3_s)
    x = L0_attn_hidden_states
    x = x + _layernorm(_L0_attn_ref(_layernorm(x, axis=-1), L0_attn_in_proj_w, L0_attn_conv_w, L0_attn_conv_b, L0_attn_x_proj_w, L0_attn_dt_proj_w, L0_attn_dt_proj_b, L0_attn_A_log, L0_attn_D_param, L0_attn_out_proj_w, L0_attn_norm_w, L0_attn_norm_f_w), axis=-1)
    x = x + _layernorm(_L0_ffn_ref(_layernorm(x, axis=-1), L0_ffn_w1_w, L0_ffn_w1_s, L0_ffn_w2_w, L0_ffn_w2_s, L0_ffn_h1_w, L0_ffn_h1_s, L0_ffn_h2_w, L0_ffn_h2_s, L0_ffn_w3_w, L0_ffn_w3_s), axis=-1)
    return x

_drawn_inputs = setup_inputs


def setup_inputs(seed=0):
    import zlib

    import numpy as np

    out = dict(_drawn_inputs(seed))
    spreads = {'L0_attn_conv_b': (0.0, 0.8),
     'L0_attn_dt_proj_b': (-4.599999904632568, 0.6),
     'L0_attn_D_param': (1.0, 0.6),
     'L0_attn_norm_w': (1.0, 0.6),
     'L0_attn_norm_f_w': (1.0, 0.2)}
    factors = {'L0_attn_in_proj_w': 7.322,
     'L0_attn_conv_w': 8.0,
     'L0_attn_x_proj_w': 8.0,
     'L0_attn_dt_proj_w': 8.0,
     'L0_attn_A_log': 8.0,
     'L0_attn_out_proj_w': 6.919}
    for name, (base, spread) in spreads.items():
        noise = np.random.default_rng([zlib.crc32(name.encode()), seed]).standard_normal(out[name].shape)
        drawn = base * np.exp(spread * noise) if base else spread * noise
        out[name] = jnp.asarray(drawn.astype(out[name].dtype))
    for name, factor in factors.items():
        out[name] = (out[name] * factor).astype(out[name].dtype)
    return out
```

```python
from contextlib import ExitStack

import concourse.bass as bass
from concourse import mybir

ALU = mybir.AluOpType
ACT = mybir.ActivationFunctionType
F32 = mybir.dt.float32

P = 128
BATCH, LENGTH, DIM = 4, 1024, 256
LAYERS, STATES, TAPS = 4, 16, 4
INNER = 2 * DIM
RANK = DIM // 16
HIDDEN = 1024
EPS = 1e-5

TOK = 512
NT = TOK // P
DC = DIM // P
EC = INNER // P
HC = HIDDEN // P
HALVES = LENGTH // TOK
GROUP = 4
NG = STATES // GROUP
STEPS = NG * EC
XD = RANK + 2 * STATES

PAIR = 2
ROUNDS = BATCH * LAYERS
PER_PAIR = PAIR * LAYERS
SLOTS = ROUNDS + (BATCH // PAIR) * PAIR

V_NORM = 0
V_CONV = V_NORM + DC
V_CBIAS = V_CONV + EC * TAPS
V_DTBIAS = V_CBIAS + EC
V_SKIP = V_DTBIAS + EC
V_ALL = V_SKIP + EC


def past(count):
    return not isinstance(count, int) or count > 0


def slot_of(rnd):
    return rnd + PAIR * (rnd // PER_PAIR)


def layer_of(rnd):
    return (rnd % PER_PAIR) // PAIR


def rows(slot, half):
    return bass.ds(slot * LENGTH + half * TOK, TOK)


def tokens_view(dram_rows):
    return dram_rows.rearrange("(t p) d -> p t d", p=P)


def make_identity(pool, ident, made):
    pool.memset(ident[:], 0.0).then_inc(made, 1)
    pool.wait_ge(made, 1)
    pool.affine_select(out=ident[:], in_=ident[:], compare_op=ALU.not_equal, fill=1.0, base=0,
                       pattern=[[-1, P]], channel_multiplier=1).then_inc(made, 1)


def normalise_input(nc, x, residual):
    units = BATCH * HALVES
    with ExitStack() as ctx:
        def sb(name, shape):
            return ctx.enter_context(nc.sbuf_tensor(name, shape, F32))

        def sem(name):
            return ctx.enter_context(nc.semaphore(name))

        xin = [sb(f"pre_x{h}", [P, NT, DIM]) for h in range(2)]
        yout = [sb(f"pre_y{h}", [P, NT, DIM]) for h in range(2)]
        stats = [sb(f"pre_stats{h}", [P, NT, 6]) for h in range(2)]
        moments = [sb(f"pre_moments{h}", [P, NT, 2]) for h in range(2)]
        var = [sb(f"pre_var{h}", [P, NT]) for h in range(2)]
        root = [sb(f"pre_root{h}", [P, NT]) for h in range(2)]
        rstd = [sb(f"pre_rstd{h}", [P, NT]) for h in range(2)]

        loaded = [sem(f"pre_loaded{h}") for h in range(2)]
        stored = [sem(f"pre_stored{h}") for h in range(2)]
        stats_done = sem("pre_stats_done")
        moments_done = sem("pre_moments_done")
        var_done = sem("pre_var_done")
        root_done = sem("pre_root_done")
        rstd_done = sem("pre_rstd_done")
        y_done = sem("pre_y_done")

        block = ctx.enter_context(nc.Block())

        @block.sync
        def _(sp):
            for u in range(units):
                h = u % 2
                if u >= 2:
                    sp.wait_ge(y_done, NT * (u - 1))
                sp.dma_start(xin[h][:], tokens_view(x[bass.ds(u * TOK, TOK), :])).then_inc(loaded[h], 16)

        @block.gpsimd
        def _(pool):
            for u in range(units):
                h = u % 2
                seq, half = u // HALVES, u % HALVES
                slot = slot_of(PER_PAIR * (seq // PAIR) + seq % PAIR)
                pool.wait_ge(y_done, NT * (u + 1))
                pool.dma_start(tokens_view(residual[rows(slot, half), :]), yout[h][:]).then_inc(stored[h], 16)
            for h in range(2):
                pool.wait_ge(stored[h], 16 * (units // 2))

        @block.scalar
        def _(act):
            for u in range(units):
                h = u % 2
                act.wait_ge(var_done, u + 1)
                act.activation(root[h][:], var[h][:], ACT.Sqrt).then_inc(root_done, 1)

        @block.vector
        def _(dve):
            for u in range(units):
                h = u % 2
                dve.wait_ge(loaded[h], 16 * (u // 2 + 1))
                for t in range(NT):
                    dve.bn_stats(stats[h][:, t, :], xin[h][:, t, :]).then_inc(stats_done, 1)
                for t in range(NT):
                    dve.wait_ge(stats_done, NT * u + t + 1)
                    dve.bn_aggr(moments[h][:, t, :], stats[h][:, t, :]).then_inc(moments_done, 1)
                dve.wait_ge(moments_done, NT * (u + 1))
                if u >= 2:
                    dve.wait_ge(root_done, u - 1)
                dve.tensor_scalar(var[h][:], moments[h][:, :, 1], EPS, None, ALU.add).then_inc(var_done, 1)
                dve.wait_ge(root_done, u + 1)
                dve.reciprocal(rstd[h][:], root[h][:]).then_inc(rstd_done, 1)
                dve.wait_ge(rstd_done, u + 1)
                if u >= 2:
                    dve.wait_ge(stored[h], 16 * (u // 2))
                for t in range(NT):
                    dve.tensor_scalar(yout[h][:, t, :], xin[h][:, t, :], moments[h][:, t, 0:1],
                                      rstd[h][:, t:t + 1], ALU.subtract, ALU.mult).then_inc(y_done, 1)


def mamba_layers(nc, residual, w_in, w_x, w_dt, w_out, vectors, a_log):
    with ExitStack() as ctx:
        def sb(name, shape):
            return ctx.enter_context(nc.sbuf_tensor(name, shape, F32))

        def sem(name):
            return ctx.enter_context(nc.semaphore(name))

        ident = sb("ident", [P, P])
        win = sb("win", [P, DC, 2 * INNER])
        wx = sb("wx", [P, EC, XD])
        wdt = sb("wdt", [RANK, INNER])
        wout = sb("wout", [P, EC, DIM])
        vec = sb("vec", [P, V_ALL])
        alog = sb("alog", [P, EC * STATES])
        aexp = sb("aexp", [P, EC * STATES])
        aneg = sb("aneg", [P, EC * STATES])
        r_a = sb("r_a", [P, NT, DIM])
        hnT = sb("hnT", [P, DC, TOK])
        neg_half, eps, per_dim = sb("neg_half", [P, NT]), sb("eps", [P, NT]), sb("per_dim", [P, NT])
        zeros = sb("zeros", [P, EC, TAPS - 1])
        ln_one = sb("ln_one", [P, 1])
        sq = sb("sq", [P, NT])
        msq = sb("msq", [P, NT])
        rs = sb("rs", [P, NT])
        xi = sb("xi", [P, EC, TAPS - 1 + TOK])
        cv = sb("cv", [P, EC, TOK])
        uu = sb("uu", [P, EC, TOK])
        skip = sb("skip", [P, EC, TOK])
        dt = [sb(f"dt{h}", [P, EC, TOK]) for h in range(2)]
        dtu = [sb(f"dtu{h}", [P, EC, TOK]) for h in range(2)]
        gate = [sb(f"gate{h}", [P, NT, INNER]) for h in range(2)]
        xdb = [sb(f"xdb{h}", [P, NT, XD]) for h in range(2)]
        dtin = sb("dtin", [RANK, TOK])
        b_all = [sb(f"b_all{i}", [P, GROUP, TOK]) for i in range(2)]
        c_all = [sb(f"c_all{i}", [P, GROUP, TOK]) for i in range(2)]
        decay = [sb(f"decay{i}", [P, GROUP, TOK]) for i in range(2)]
        hx = [sb(f"hx{c}", [P, GROUP, TOK]) for c in range(EC)]
        hlast = sb("hlast", [P, EC * STATES])
        yg = [sb(f"yg{i}", [P, NT, P]) for i in range(2)]
        ygT = sb("ygT", [P, EC, TOK])
        r_c = sb("r_c", [P, NT, DIM])

        ysum = [ctx.enter_context(nc.psum_tensor(f"ysum{c}", [P, TOK], F32)) for c in range(EC)]
        pq = [ctx.enter_context(nc.psum_tensor(f"pq{i}", [P, TOK], F32)) for i in range(2)]
        pp = [ctx.enter_context(nc.psum_tensor(f"pp{i}", [P, TOK], F32)) for i in range(2)]

        ident_made, ln_one_made = sem("ident_made"), sem("ln_one_made")
        win_loaded, wx_loaded, wout_loaded = sem("win_loaded"), sem("wx_loaded"), sem("wout_loaded")
        vec_loaded, alog_loaded = sem("vec_loaded"), sem("alog_loaded")
        ra_loaded, rc_loaded, r_stored = sem("ra_loaded"), sem("rc_loaded"), sem("r_stored")
        hnT_full, xi_full, z_full, xdb_full = sem("hnT_full"), sem("xi_full"), sem("z_full"), sem("xdb_full")
        dtin_full, dt_full, bc_full = sem("dtin_full"), sem("dt_full"), sem("bc_full")
        ysum_done, back_full, out_full = sem("ysum_done"), sem("back_full"), sem("out_full")
        aneg_made, sq_made = sem("aneg_made"), sem("sq_made")
        hnT_made, xi_made, u_made, gate_made = sem("hnT_made"), sem("xi_made"), sem("u_made"), sem("gate_made")
        xdb_made, dtin_made, xb_made = sem("xdb_made"), sem("dtin_made"), sem("xb_made")
        abs_made, e_made, ln_made, skip_made = sem("abs_made"), sem("e_made"), sem("ln_made"), sem("skip_made")
        decay_made, b_made, c_made, ygT_made = sem("decay_made"), sem("b_made"), sem("c_made"), sem("ygT_made")
        scan_done, hlast_saved, hc_made = sem("scan_done"), sem("hlast_saved"), sem("hc_made")
        conv_done, rest_steps, rest_made = sem("conv_done"), sem("rest_steps"), sem("rest_made")
        dt_made = sem("dt_made")
        yg_made, r_made = sem("yg_made"), sem("r_made")
        rs_made, hn_made, lead_made = sem("rs_made"), sem("hn_made"), sem("lead_made")
        dtu_made, inject_made = sem("dtu_made"), sem("inject_made")

        block = ctx.enter_context(nc.Block())


        @block.sync
        def _(sp):
            def load_prep_weights(j):
                v = 2 * j - 1
                lay = layer_of(j)
                if past(v):
                    sp.wait_ge(z_full, 4 * (v + 1))
                sp.dma_start(win[:], w_in[lay].rearrange("(c p) e -> p c e", p=P)).then_inc(win_loaded, 16)
                if past(v):
                    sp.wait_ge(dt_full, 4 * (v + 1))
                sp.dma_start(wx[:], w_x[lay].rearrange("(c p) r -> p c r", p=P)).then_inc(wx_loaded, 16)
                sp.dma_start(wdt[:], w_dt[lay]).then_inc(wx_loaded, 16)
                if past(v):
                    sp.wait_ge(skip_made, EC * (v + 1))
                sp.dma_start(vec[:], vectors[lay]).then_inc(vec_loaded, 16)

            def load_alog(j):
                if past(j):
                    sp.wait_ge(aneg_made, 2 * (j - 1) + 1)
                sp.dma_start(alog[:], a_log[layer_of(j)]).then_inc(alog_loaded, 16)

            def load_ra(j, h):
                v = 2 * j + h
                if past(v):
                    sp.wait_ge(hnT_full, DC * v)
                if past(v - 3):
                    sp.wait_ge(r_stored, 16 * (v - 3))
                sp.dma_start(r_a[:], tokens_view(residual[rows(slot_of(j), h), :])).then_inc(ra_loaded, 16)

            def load_rc(j, h):
                w = 2 * j + h
                if past(w):
                    sp.wait_ge(r_stored, 16 * w)
                sp.dma_start(r_c[:], tokens_view(residual[rows(slot_of(j), h), :])).then_inc(rc_loaded, 16)

            def store(j, h):
                w = 2 * j + h
                sp.wait_ge(r_made, 2 * (w + 1))
                sp.dma_start(tokens_view(residual[rows(slot_of(j) + PAIR, h), :]), r_c[:]).then_inc(r_stored, 16)

            def stage(j, h, first=False, last=False):
                u = 2 * j + h
                if not first:
                    load_rc(j + h - 1, 1 - h)
                if not last:
                    load_ra(j + h, 1 - h)
                if h == 1 and not last:
                    load_alog(j + 1)
                if not first:
                    store(j + h - 1, 1 - h)
                if h == 0:
                    if not first:
                        sp.wait_ge(out_full, 2 * u)
                    sp.dma_start(wout[:], w_out[layer_of(j)].rearrange("(c p) d -> p c d", p=P)).then_inc(wout_loaded, 16)
                    if not isinstance(j, int) or j + 1 < ROUNDS:
                        load_prep_weights(j + 1)

            load_prep_weights(0)
            load_alog(0)
            load_ra(0, 0)
            stage(0, 0, first=True)
            stage(0, 1)
            with sp.Fori(1, ROUNDS - 1) as j:
                stage(j, 0)
                stage(j, 1)
            stage(ROUNDS - 1, 0)
            stage(ROUNDS - 1, 1, last=True)
            load_rc(ROUNDS - 1, 1)
            store(ROUNDS - 1, 1)
            sp.wait_ge(r_stored, 16 * 2 * ROUNDS)

        @block.tensor
        def _(pe):
            def norm_transposes(j, h):
                v = 2 * j + h
                pe.wait_ge(hn_made, v + 1)
                for c in range(DC):
                    if past(v - 1):
                        pe.wait_ge(r_made, 2 * (v - 2) + c + 1)
                    elif past(v):
                        pe.wait_ge(xb_made, EC * (v - 1) + 2 + c + 1)
                    for t in range(NT):
                        i = pe.transpose(pp[c][:, t * P:(t + 1) * P], r_a[:, t, c * P:(c + 1) * P], ident[:])
                    i.then_inc(hnT_full, 1)

            def in_projection_x(j, h, tiles):
                v = 2 * j + h
                pe.wait_ge(hnT_made, DC * (v + 1))
                pe.wait_ge(win_loaded, 16 * (j + 1))
                for c in tiles:
                    if c >= 2:
                        pe.wait_ge(xi_made, 2 * (EC * v + c - 2 + 1))
                    for k in range(DC):
                        i = pe.matmul(pp[c % 2][:], win[:, k, c * P:(c + 1) * P], hnT[:, k, :],
                                      start=(k == 0), stop=(k == DC - 1))
                    i.then_inc(xi_full, 1)

            def in_projection_z(j, h, tiles):
                v = 2 * j + h
                for t in tiles:
                    if t < 2:
                        pe.wait_ge(xi_made, 2 * (EC * v + t + 2 + 1))
                    else:
                        pe.wait_ge(gate_made, NT * v + t - 2 + 1)
                    for k in range(DC):
                        i = pe.matmul(pp[t % 2][:], hnT[:, k, t * P:(t + 1) * P], win[:, k, INNER:2 * INNER],
                                      start=(k == 0), stop=(k == DC - 1))
                    i.then_inc(z_full, 1)

            def x_projection(j, h):
                v = 2 * j + h
                pe.wait_ge(u_made, v + 1)
                pe.wait_ge(wx_loaded, 32 * (j + 1))
                pe.wait_ge(gate_made, NT * v + 3)
                for t in range(NT):
                    for c in range(EC):
                        i = pe.matmul(pp[0][:, t * XD:(t + 1) * XD], uu[:, c, t * P:(t + 1) * P], wx[:, c, :],
                                      start=(c == 0), stop=(c == EC - 1))
                i.then_inc(xdb_full, 1)

            def dt_transposes(j, h):
                v = 2 * j + h
                pe.wait_ge(xdb_made, v + 1)
                pe.wait_ge(gate_made, NT * v + 4)
                for t in range(NT):
                    i = pe.transpose(pp[1][0:RANK, t * P:(t + 1) * P], xdb[h][:, t, 0:RANK], ident[:])
                i.then_inc(dtin_full, 1)

            def dt_projection(j, h):
                v = 2 * j + h
                pe.wait_ge(dtin_made, v + 1)
                for c in range(EC):
                    if c >= 2:
                        pe.wait_ge(xb_made, EC * v + c - 2 + 1)
                    pe.matmul(pp[c % 2][:], wdt[:, c * P:(c + 1) * P], dtin[:], start=True,
                              stop=True).then_inc(dt_full, 1)

            def spread(v, h, g, i):
                n = i % GROUP
                col = RANK + (STATES if i >= GROUP else 0) + GROUP * g + n
                if i < 2:
                    if past(STATES * v + GROUP * g):
                        pe.wait_ge(c_made, STATES * v + GROUP * g + i - 1)
                elif i < 2 + GROUP:
                    pe.wait_ge(b_made, STATES * v + GROUP * g + i - 2 + 1)
                else:
                    pe.wait_ge(c_made, STATES * v + GROUP * g + i - 2 - GROUP + 1)
                if g == 0 and i == 0:
                    pe.wait_ge(xdb_made, v + 1)
                for t in range(NT):
                    ins = pe.transpose(pq[i % 2][:, t * P:(t + 1) * P],
                                       xdb[h][:, t, col:col + 1].to_broadcast([P, P]), ident[:])
                ins.then_inc(bc_full, 1)

            def sum_states(u, k):
                g, c = k // EC, k % EC
                if g == 0:
                    if past(u):
                        pe.wait_ge(yg_made, EC * (u - 1) + c + 1)
                    pe.wait_ge(skip_made, EC * (u + 1))
                    for t in range(NT):
                        pe.matmul(ysum[c][:, t * P:(t + 1) * P], skip[:, c, t * P:(t + 1) * P], ident[:],
                                  is_transpose=True, start=(t == 0), stop=False, skip_group_check=True)
                pe.wait_ge(hc_made, STEPS * u + k + 1)
                for n in range(GROUP):
                    for t in range(NT):
                        i = pe.matmul(ysum[c][:, t * P:(t + 1) * P], hx[c][:, n, t * P:(t + 1) * P], ident[:],
                                      is_transpose=True, start=False, stop=(g == NG - 1 and n == GROUP - 1),
                                      skip_group_check=True)
                i.then_inc(ysum_done, 1)

            def back_transposes(w, c, last=False):
                pe.wait_ge(yg_made, EC * w + c + 1)
                if c >= 2:
                    pe.wait_ge(ygT_made, EC * w + c - 2 + 1)
                elif last:
                    pe.wait_ge(r_made, 2 * (w - 1) + c + 1)
                else:
                    pe.wait_ge(xb_made, EC * (w + 1) + 2 + c + 1)
                for t in range(NT):
                    i = pe.transpose(pp[c % 2][:, t * P:(t + 1) * P], yg[c % 2][:, t, :], ident[:])
                i.then_inc(back_full, 1)

            def out_projection(j, h):
                w = 2 * j + h
                pe.wait_ge(ygT_made, EC * (w + 1))
                pe.wait_ge(wout_loaded, 16 * (j + 1))
                for i2 in range(2):
                    for t in range(2):
                        for c in range(EC):
                            tok = (2 * i2 + t) * P
                            i = pe.matmul(pp[i2][:, t * DIM:(t + 1) * DIM], ygT[:, c, tok:tok + P], wout[:, c, :],
                                          start=(c == 0), stop=(c == EC - 1))
                    i.then_inc(out_full, 1)

            def stage(j, h, first=False, last=False):
                u = 2 * j + h
                jv, hv = j + h, 1 - h
                jw, hw = j + h - 1, 1 - h
                for k in range(STEPS):
                    g = k // EC
                    for i in range(2 * (k % EC), 2 * (k % EC) + 2):
                        if g < NG - 1:
                            spread(u, h, g + 1, i)
                        elif not last:
                            spread(u + 1, hv, 0, i)
                    if k < 3 and not first:
                        back_transposes(u - 1, k + 1, last)
                    if k == 3 and not first:
                        out_projection(jw, hw)
                    if not last:
                        if k == 4:
                            norm_transposes(jv, hv)
                        if k == 5:
                            in_projection_x(jv, hv, (0, 1))
                        if k == 6:
                            in_projection_x(jv, hv, (2, 3))
                        if k == 7:
                            in_projection_z(jv, hv, (0, 1))
                        if k == 8:
                            in_projection_z(jv, hv, (2, 3))
                        if k == 9:
                            x_projection(jv, hv)
                        if k == 10:
                            dt_transposes(jv, hv)
                        if k == 11:
                            dt_projection(jv, hv)
                    if k == 15:
                        back_transposes(u, 0, last)
                    if k > 0:
                        sum_states(u, k - 1)
                    elif not first:
                        sum_states(u - 1, STEPS - 1)

            pe.wait_ge(ident_made, 2)
            norm_transposes(0, 0)
            in_projection_x(0, 0, range(EC))
            in_projection_z(0, 0, range(NT))
            x_projection(0, 0)
            dt_transposes(0, 0)
            dt_projection(0, 0)
            for i in range(2 * GROUP):
                spread(0, 0, 0, i)
            stage(0, 0, first=True)
            stage(0, 1)
            with pe.Fori(1, ROUNDS - 1) as j:
                stage(j, 0)
                stage(j, 1)
            stage(ROUNDS - 1, 0)
            stage(ROUNDS - 1, 1, last=True)
            sum_states(2 * ROUNDS - 1, STEPS - 1)
            for c in range(1, EC):
                back_transposes(2 * ROUNDS - 1, c, last=True)
            out_projection(ROUNDS - 1, 1)

        @block.scalar
        def _(act):
            def square_sums(j, h):
                v = 2 * j + h
                act.wait_ge(ra_loaded, 16 * (v + 1))
                if past(v):
                    act.wait_ge(z_full, NT * v)
                    act.wait_ge(rs_made, 3 * v)
                for t in range(NT):
                    act.activation(hnT[:, t // 2, t % 2 * DIM:(t % 2 + 1) * DIM], r_a[:, t, :], ACT.Square,
                                   accum_out=sq[:, t:t + 1]).then_inc(sq_made, 1)

            def take_hnT(j, h):
                v = 2 * j + h
                act.wait_ge(vec_loaded, 16 * (j + 1))
                if past(v):
                    act.wait_ge(z_full, NT * v)
                for c in range(DC):
                    act.wait_ge(hnT_full, DC * v + c + 1)
                    act.activation(hnT[:, c, :], pp[c][:], ACT.Copy,
                                   scale=vec[:, V_NORM + c:V_NORM + c + 1]).then_inc(hnT_made, 1)

            def take_xi(j, h, tiles):
                v = 2 * j + h
                act.wait_ge(lead_made, v + 1)
                if past(v):
                    act.wait_ge(rest_made, v)
                for c in tiles:
                    act.wait_ge(xi_full, EC * v + c + 1)
                    act.activation(xi[:, c, TAPS - 1:], pp[c % 2][:], ACT.Copy).then_inc(xi_made, 1)
                    tap = V_CONV + c * TAPS + TAPS - 1
                    act.activation(cv[:, c, :], pp[c % 2][:], ACT.Identity, scale=vec[:, tap:tap + 1],
                                   bias=vec[:, V_CBIAS + c:V_CBIAS + c + 1]).then_inc(xi_made, 1)

            def silus(j, h):
                v = 2 * j + h
                if past(v - 1):
                    act.wait_ge(yg_made, EC * (v - 1))
                for t in range(NT):
                    act.wait_ge(z_full, NT * v + t + 1)
                    act.activation(gate[h][:, t, :], pp[t % 2][:], ACT.Silu).then_inc(gate_made, 1)
                act.wait_ge(conv_done, EC * (TAPS - 1) * (v + 1))
                if past(v):
                    act.wait_ge(dtu_made, EC * v)
                    act.wait_ge(skip_made, EC * v)
                    act.wait_ge(xdb_full, v)
                act.activation(uu[:], cv[:], ACT.Silu).then_inc(u_made, 1)
                act.preload_act_table_set("natural_log_exp_and_others")

            def take_xdb(j, h):
                v = 2 * j + h
                act.wait_ge(xdb_full, v + 1)
                if past(v - 1):
                    act.wait_ge(c_made, STATES * (v - 1))
                act.activation(xdb[h][:].rearrange("p t r -> p (t r)"), pp[0][:, 0:NT * XD],
                               ACT.Copy).then_inc(xdb_made, 1)

            def take_dtin(j, h):
                v = 2 * j + h
                act.wait_ge(dtin_full, v + 1)
                if past(v):
                    act.wait_ge(dt_full, EC * v)
                act.activation(dtin[:], pp[1][0:RANK, :], ACT.Copy).then_inc(dtin_made, 1)

            def take_dt(j, h):
                v = 2 * j + h
                act.wait_ge(u_made, v + 1)
                for c in range(EC):
                    act.wait_ge(dt_full, EC * v + c + 1)
                    act.activation(cv[:, c, :], pp[c % 2][:], ACT.Identity,
                                   bias=vec[:, V_DTBIAS + c:V_DTBIAS + c + 1]).then_inc(xb_made, 1)

            def softplus_exp(j, h):
                v = 2 * j + h
                act.wait_ge(xb_made, EC * (v + 1))
                if past(v - 1):
                    act.wait_ge(inject_made, STEPS * (v - 1))
                act.activation(dtu[h][:], cv[:], ACT.Abs).then_inc(abs_made, 1)
                act.wait_ge(abs_made, v + 1)
                act.activation(dtu[h][:], dtu[h][:], ACT.Exp, scale=-1.0).then_inc(e_made, 1)

            def softplus_ln(j, h):
                v = 2 * j + h
                act.wait_ge(e_made, v + 1)
                if past(v - 1):
                    act.wait_ge(decay_made, GROUP * STEPS * (v - 1))
                    act.wait_ge(dtu_made, EC * (v - 1))
                act.activation(dt[h][:], dtu[h][:], ACT.Ln, bias=1.0).then_inc(ln_made, 1)

            def skips(j, h):
                v = 2 * j + h
                act.wait_ge(dt_made, v + 1)
                act.wait_ge(u_made, v + 1)
                for c in range(EC):
                    act.activation(skip[:, c, :], uu[:, c, :], ACT.Copy,
                                   scale=vec[:, V_SKIP + c:V_SKIP + c + 1]).then_inc(skip_made, 1)

            def make_aneg(j):
                u = 2 * j
                act.wait_ge(alog_loaded, 16 * (j + 1))
                if past(u):
                    act.wait_ge(decay_made, GROUP * STEPS * u)
                act.activation(aexp[:], alog[:], ACT.Exp).then_inc(aneg_made, 1)
                act.wait_ge(aneg_made, 2 * j + 1)
                act.activation(aneg[:], aexp[:], ACT.Copy, scale=-1.0).then_inc(aneg_made, 1)
                act.wait_ge(aneg_made, 2 * j + 2)

            def decays(u, h, k):
                g, c = k // EC, k % EC
                if k == 0:
                    act.wait_ge(dt_made, u + 1)
                if past(STEPS * u + k - 1):
                    act.wait_ge(scan_done, STEPS * u + k - 1)
                for n in range(GROUP):
                    col = c * STATES + g * GROUP + n
                    act.activation(decay[k % 2][:, n, :], dt[h][:, c, :], ACT.Exp,
                                   scale=aneg[:, col:col + 1]).then_inc(decay_made, 1)

            def take_spread(v, g, i):
                act.wait_ge(bc_full, 2 * STATES * v + 2 * GROUP * g + i + 1)
                n = i % GROUP
                done = STEPS * v + EC * (g - 1)
                if i < GROUP:
                    if past(done):
                        act.wait_ge(inject_made, done)
                    act.activation(b_all[g % 2][:, n, :], pq[i % 2][:], ACT.Copy).then_inc(b_made, 1)
                else:
                    if past(done):
                        act.wait_ge(hc_made, done)
                    act.activation(c_all[g % 2][:, n, :], pq[i % 2][:], ACT.Copy).then_inc(c_made, 1)

            def take_back(w, c):
                act.wait_ge(back_full, EC * w + c + 1)
                if past(w):
                    act.wait_ge(out_full, 2 * w)
                act.activation(ygT[:, c, :], pp[c % 2][:], ACT.Copy).then_inc(ygT_made, 1)

            def stage(j, h, first=False, last=False):
                u = 2 * j + h
                jv, hv = j + h, 1 - h
                for k in range(STEPS):
                    g = k // EC
                    if k < STEPS - 1:
                        decays(u, h, k + 1)
                    elif not last:
                        if h == 1:
                            make_aneg(j + 1)
                        decays(u + 1, hv, 0)
                    for i in range(2 * (k % EC), 2 * (k % EC) + 2):
                        if g < NG - 1:
                            take_spread(u, g + 1, i)
                        elif not last:
                            take_spread(u + 1, 0, i)
                    if k < 3 and not first:
                        take_back(u - 1, k + 1)
                    if not last:
                        if k == 0:
                            square_sums(jv, hv)
                        if k == 4:
                            take_hnT(jv, hv)
                        if k == 5:
                            take_xi(jv, hv, (0, 1))
                        if k == 6:
                            take_xi(jv, hv, (2, 3))
                        if k == 8:
                            silus(jv, hv)
                        if k == 9:
                            take_xdb(jv, hv)
                        if k == 10:
                            take_dtin(jv, hv)
                        if k == 11:
                            take_dt(jv, hv)
                        if k == 12:
                            softplus_exp(jv, hv)
                        if k == 13:
                            softplus_ln(jv, hv)
                        if k == 15:
                            skips(jv, hv)
                    if k == 15:
                        take_back(u, 0)

            act.preload_act_table_set("natural_log_exp_and_others")
            act.wait_ge(ident_made, 6)
            act.activation(ln_one[:], zeros[:, 0, 0:1], ACT.Ln, bias=1.0).then_inc(ln_one_made, 1)
            square_sums(0, 0)
            take_hnT(0, 0)
            take_xi(0, 0, range(EC))
            silus(0, 0)
            take_xdb(0, 0)
            take_dtin(0, 0)
            take_dt(0, 0)
            softplus_exp(0, 0)
            softplus_ln(0, 0)
            skips(0, 0)
            for i in range(2 * GROUP):
                take_spread(0, 0, i)
            make_aneg(0)
            decays(0, 0, 0)
            stage(0, 0, first=True)
            stage(0, 1)
            with act.Fori(1, ROUNDS - 1) as j:
                stage(j, 0)
                stage(j, 1)
            stage(ROUNDS - 1, 0)
            stage(ROUNDS - 1, 1, last=True)
            for c in range(1, EC):
                take_back(2 * ROUNDS - 1, c)

        @block.vector
        def _(dve):
            def convolve(j, h, pair):
                v = 2 * j + h
                done = EC * (TAPS - 1) * v + 2 * (TAPS - 1) * pair
                for tap in range(TAPS - 1):
                    for c in (2 * pair, 2 * pair + 1):
                        if tap == 0:
                            dve.wait_ge(xi_made, 2 * (EC * v + c + 1))
                        else:
                            dve.wait_ge(conv_done, done + 2 * (tap - 1) + c - 2 * pair + 1)
                        col = V_CONV + c * TAPS + tap
                        dve.scalar_tensor_tensor(out=cv[:, c, :], in0=xi[:, c, tap:tap + TOK],
                                                 scalar=vec[:, col:col + 1], in1=cv[:, c, :],
                                                 op0=ALU.mult, op1=ALU.add).then_inc(conv_done, 1)

            def softplus_rest(j, h):
                v = 2 * j + h
                dve.wait_ge(e_made, v + 1)
                if past(v):
                    dve.wait_ge(ysum_done, STEPS * (v - 1) + EC)
                dve.tensor_scalar(skip[:], dtu[h][:], 1.0, None, ALU.add).then_inc(rest_steps, 1)
                dve.wait_ge(rest_steps, 2 * v + 1)
                dve.scalar_tensor_tensor(out=skip[:], in0=skip[:], scalar=1.0, in1=dtu[h][:],
                                         op0=ALU.subtract, op1=ALU.subtract).then_inc(rest_steps, 1)

            def softplus_linear(j, h):
                v = 2 * j + h
                dve.wait_ge(rest_steps, 2 * v + 2)
                dve.scalar_tensor_tensor(out=skip[:], in0=cv[:], scalar=0.0, in1=skip[:],
                                         op0=ALU.max, op1=ALU.subtract).then_inc(rest_made, 1)

            def softplus_sum(j, h):
                v = 2 * j + h
                dve.wait_ge(rest_made, v + 1)
                dve.wait_ge(ln_made, v + 1)
                dve.scalar_tensor_tensor(out=dt[h][:], in0=dt[h][:], scalar=ln_one[:, 0:1], in1=skip[:],
                                         op0=ALU.subtract, op1=ALU.add).then_inc(dt_made, 1)

            def recur(j, h, k):
                u = 2 * j + h
                g, c = k // EC, k % EC
                state = slice(c * STATES + g * GROUP, c * STATES + (g + 1) * GROUP)
                dve.wait_ge(inject_made, STEPS * u + k + 1)
                if h == 1:
                    dve.wait_ge(hlast_saved, STEPS * j + k + 1)
                for n in range(GROUP):
                    dve.wait_ge(decay_made, GROUP * (STEPS * u + k) + n + 1)
                    start = hlast[:, state.start + n:state.start + n + 1] if h else 0.0
                    i = dve.tensor_tensor_scan(hx[c][:, n, :], decay[k % 2][:, n, :], hx[c][:, n, :], start,
                                               ALU.mult, ALU.add)
                i.then_inc(scan_done, 1)
                dve.wait_ge(scan_done, STEPS * u + k + 1)
                if h == 0:
                    dve.tensor_copy(hlast[:, state], hx[c][:, :, TOK - 1]).then_inc(hlast_saved, 1)
                    dve.wait_ge(hlast_saved, STEPS * j + k + 1)
                dve.wait_ge(c_made, STATES * u + GROUP * (g + 1))
                dve.tensor_tensor(hx[c][:], hx[c][:], c_all[g % 2][:], ALU.mult).then_inc(hc_made, 1)

            def gate_output(w, h, c):
                dve.wait_ge(ysum_done, STEPS * w + (NG - 1) * EC + c + 1)
                dve.wait_ge(gate_made, NT * (w + 1))
                if past(EC * w + c - 1):
                    dve.wait_ge(back_full, EC * w + c - 1)
                dve.tensor_tensor(yg[c % 2][:], ysum[c][:].rearrange("p (t e) -> p t e", e=P),
                                  gate[h][:, :, c * P:(c + 1) * P], ALU.mult).then_inc(yg_made, 1)

            def add_residual(j, h):
                w = 2 * j + h
                dve.wait_ge(rc_loaded, 16 * (w + 1))
                for i in range(2):
                    dve.wait_ge(out_full, 2 * w + i + 1)
                    part = r_c[:, 2 * i:2 * i + 2, :]
                    dve.tensor_tensor(part, part, pp[i][:].rearrange("p (t d) -> p t d", d=DIM),
                                      ALU.add).then_inc(r_made, 1)

            def stage(j, h, first=False, last=False):
                u = 2 * j + h
                jv, hv = j + h, 1 - h
                for k in range(STEPS):
                    recur(j, h, k)
                    if k < 2 and not first:
                        gate_output(u - 1, 1 - h, k + 2)
                    if k == 3 and not first:
                        add_residual(j + h - 1, 1 - h)
                    if not last:
                        if k == 6:
                            convolve(jv, hv, 0)
                        if k == 7:
                            convolve(jv, hv, 1)
                        if k == 13:
                            softplus_rest(jv, hv)
                        if k == 14:
                            softplus_linear(jv, hv)
                            softplus_sum(jv, hv)
                    if k >= 14:
                        gate_output(u, h, k - 14)

            convolve(0, 0, 0)
            convolve(0, 0, 1)
            softplus_rest(0, 0)
            softplus_linear(0, 0)
            dve.wait_ge(ln_one_made, 1)
            softplus_sum(0, 0)
            stage(0, 0, first=True)
            stage(0, 1)
            with dve.Fori(1, ROUNDS - 1) as j:
                stage(j, 0)
                stage(j, 1)
            stage(ROUNDS - 1, 0)
            stage(ROUNDS - 1, 1, last=True)
            gate_output(2 * ROUNDS - 1, 1, 2)
            gate_output(2 * ROUNDS - 1, 1, 3)
            add_residual(ROUNDS - 1, 1)

        @block.gpsimd
        def _(pool):
            def normalise(j, h):
                v = 2 * j + h
                pool.wait_ge(sq_made, NT * (v + 1))
                if past(v):
                    pool.wait_ge(hn_made, v)
                pool.tensor_tensor(msq[:], sq[:], per_dim[:], ALU.mult).then_inc(rs_made, 1)
                pool.wait_ge(rs_made, 3 * v + 1)
                pool.tensor_tensor(msq[:], msq[:], eps[:], ALU.add).then_inc(rs_made, 1)
                pool.wait_ge(rs_made, 3 * v + 2)
                pool.tensor_tensor(rs[:], msq[:], neg_half[:], ALU.pow).then_inc(rs_made, 1)
                pool.wait_ge(rs_made, 3 * v + 3)
                pool.tensor_tensor(r_a[:], r_a[:], rs[:].rearrange("p (t a) -> p t a", a=1).to_broadcast([P, NT, DIM]),
                                   ALU.mult).then_inc(hn_made, 1)

            def lead(j, h):
                v = 2 * j + h
                if past(v):
                    pool.wait_ge(conv_done, EC * (TAPS - 1) * v)
                before = xi[:, :, TOK:TOK + TAPS - 1] if h == 1 else zeros[:]
                pool.tensor_tensor(xi[:, :, 0:TAPS - 1], before, zeros[:], ALU.add).then_inc(lead_made, 1)

            def make_dtu(v, h, c):
                pool.wait_ge(dt_made, v + 1)
                pool.wait_ge(u_made, v + 1)
                pool.tensor_tensor(dtu[h][:, c, :], dt[h][:, c, :], uu[:, c, :], ALU.mult).then_inc(dtu_made, 1)

            def inject(u, h, k):
                g, c = k // EC, k % EC
                if g == 0:
                    make_dtu(u, h, c)
                    pool.wait_ge(dtu_made, EC * u + c + 1)
                pool.wait_ge(b_made, STATES * u + GROUP * (g + 1))
                if past(STEPS * u + k - EC + 1):
                    pool.wait_ge(ysum_done, STEPS * u + k - EC + 1)
                pool.tensor_tensor(hx[c][:], dtu[h][:, c:c + 1, :].to_broadcast([P, GROUP, TOK]), b_all[g % 2][:],
                                   ALU.mult).then_inc(inject_made, 1)

            def stage(j, h, first=False, last=False):
                u = 2 * j + h
                jv, hv = j + h, 1 - h
                for k in range(STEPS):
                    inject(u, h, k)
                    if not last:
                        if k == 2:
                            normalise(jv, hv)
                        if k == 3:
                            lead(jv, hv)

            make_identity(pool, ident, ident_made)
            for tile, value in ((neg_half, -0.5), (eps, EPS), (per_dim, 1.0 / DIM), (zeros, 0.0)):
                pool.memset(tile[:], value).then_inc(ident_made, 1)
            pool.wait_ge(ident_made, 6)
            normalise(0, 0)
            lead(0, 0)
            stage(0, 0, first=True)
            stage(0, 1)
            with pool.Fori(1, ROUNDS - 1) as j:
                stage(j, 0)
                stage(j, 1)
            stage(ROUNDS - 1, 0)
            stage(ROUNDS - 1, 1, last=True)


def feed_forward(nc, x, residual, norm_f, w1, w2, h1, h2, w3, scales, w3_scale, out):
    units = BATCH * HALVES
    LN_ATT, LN_IN, LN_OUT = range(3)
    GATE, UP, MID1, MID2 = range(4)
    with ExitStack() as ctx:
        def sb(name, shape):
            return ctx.enter_context(nc.sbuf_tensor(name, shape, F32))

        def psum(name):
            return ctx.enter_context(nc.psum_tensor(name, [P, TOK], F32))

        def sem(name):
            return ctx.enter_context(nc.semaphore(name))

        ident = sb("f_ident", [P, P])
        neg_half, eps, per_dim = sb("f_neg_half", [P, NT]), sb("f_eps", [P, NT]), sb("f_per_dim", [P, NT])
        spare = sb("f_spare", [P, 1])
        w1_sb = sb("w1_sb", [P, DC, HIDDEN])
        w2_sb = sb("w2_sb", [P, DC, HIDDEN])
        h1_sb = sb("h1_sb", [P, HC, HIDDEN])
        h2_sb = sb("h2_sb", [P, HC, HIDDEN])
        w3_sb = sb("w3_sb", [P, HC, DIM])
        sc_sb = sb("sc_sb", [P, 4, HC])
        s3_sb = sb("s3_sb", [P, DIM])
        nf_sb = sb("nf_sb", [P, DIM])
        r_in = sb("f_r", [P, NT, DIM])
        x_in = sb("f_x", [P, NT, DIM])
        x1_next = sb("f_x1_next", [P, NT, DIM])
        x1 = sb("f_x1", [P, NT, DIM])
        y = sb("f_y", [P, NT, DIM])
        yT = sb("f_yT", [P, DC, TOK])
        ha = sb("f_ha", [P, HC, TOK])
        hb = sb("f_hb", [P, HC, TOK])
        hc = sb("f_hc", [P, HC, TOK])
        o_sb = sb("f_o", [P, NT, DIM])
        sq = sb("f_sq", [P, NT])
        msq = sb("f_msq", [P, NT])
        rms = sb("f_rms", [P, NT])
        stats = [sb(f"f_stats{i}", [P, NT, 6]) for i in range(3)]
        mom = [sb(f"f_mom{i}", [P, NT, 2]) for i in range(3)]
        var = [sb(f"f_var{i}", [P, NT]) for i in range(3)]
        rstd = [sb(f"f_rstd{i}", [P, NT]) for i in range(3)]

        pm = [psum(f"pm{i}") for i in range(4)]
        pt = [psum(f"pt{i}") for i in range(2)]
        po = [psum(f"po{i}") for i in range(2)]

        made = sem("f_made")
        w12_loaded, h1_loaded, h2_loaded, w3_loaded = (sem(f"f_{n}_loaded") for n in ("w12", "h1", "h2", "w3"))
        small_loaded = sem("f_small_loaded")
        r_loaded, x_loaded, out_stored = sem("f_r_loaded"), sem("f_x_loaded"), sem("f_out_stored")
        sq_made, msq_made, rms_made = sem("f_sq_made"), sem("f_msq_made"), sem("f_rms_made")
        stats_made = [sem(f"f_stats_made{i}") for i in range(3)]
        mom_made = [sem(f"f_mom_made{i}") for i in range(3)]
        var_made = [sem(f"f_var_made{i}") for i in range(3)]
        rstd_made = [sem(f"f_rstd_made{i}") for i in range(3)]
        att_scaled, att_normed, x1_made, y_made = (sem(f"f_{n}") for n in ("att_scaled", "att_normed", "x1_made", "y_made"))
        x1_moved = sem("f_x1_moved")
        yT_full, yT_made = sem("f_yT_full"), sem("f_yT_made")
        gate_full, up_full, mid1_full, mid2_full = (sem(f"f_{n}_full") for n in ("gate", "up", "mid1", "mid2"))
        silu_made, ha_made, hb_made, hc_made = (sem(f"f_{n}_made") for n in ("silu", "ha", "hb", "hc"))
        o_full, o_scaled, o_normed, o_made = (sem(f"f_{n}") for n in ("o_full", "o_scaled", "o_normed", "o_made"))

        block = ctx.enter_context(nc.Block())

        def res_rows(u):
            seq = u // HALVES
            pair = seq // PAIR
            return rows((pair + 1) * (PER_PAIR + PAIR) - PAIR + seq % PAIR, u % HALVES)

        @block.sync
        def _(sp):
            def load(u):
                if past(u):
                    sp.wait_ge(x1_made, u)
                sp.dma_start(r_in[:], tokens_view(residual[res_rows(u), :])).then_inc(r_loaded, 16)
                sp.dma_start(x_in[:], tokens_view(x[bass.ds(u * TOK, TOK), :])).then_inc(x_loaded, 16)

            def store(u):
                sp.wait_ge(o_made, u + 1)
                sp.dma_start(tokens_view(out[bass.ds(u * TOK, TOK), :]), o_sb[:]).then_inc(out_stored, 16)

            load(0)
            sp.dma_start(w1_sb[:], w1.rearrange("(c p) o -> p c o", p=P)).then_inc(w12_loaded, 16)
            sp.dma_start(w2_sb[:], w2.rearrange("(c p) o -> p c o", p=P)).then_inc(w12_loaded, 16)
            sp.dma_start(h1_sb[:], h1.rearrange("(c p) o -> p c o", p=P)).then_inc(h1_loaded, 16)
            sp.dma_start(h2_sb[:], h2.rearrange("(c p) o -> p c o", p=P)).then_inc(h2_loaded, 16)
            sp.dma_start(w3_sb[:], w3.rearrange("(c p) o -> p c o", p=P)).then_inc(w3_loaded, 16)
            load(1)
            with sp.Fori(0, units - 2) as u:
                load(u + 2)
                store(u)
            store(units - 2)
            store(units - 1)
            sp.wait_ge(out_stored, 16 * units)

        @block.tensor
        def _(pe):
            def transposes(u):
                pe.wait_ge(y_made, NT * (u + 1))
                if past(u):
                    pe.wait_ge(yT_made, DC * u)
                for c in range(DC):
                    for t in range(NT):
                        i = pe.transpose(pt[c][:, t * P:(t + 1) * P], y[:, t, c * P:(c + 1) * P], ident[:])
                    i.then_inc(yT_full, 1)

            def gated_layers(u):
                pe.wait_ge(yT_made, DC * (u + 1))
                pe.wait_ge(w12_loaded, 32)
                for o in range(HC):
                    gate, up = pm[2 * o % 4], pm[(2 * o + 1) % 4]
                    if o >= 2:
                        pe.wait_ge(ha_made, HC * u + o - 2 + 1)
                    elif past(u):
                        pe.wait_ge(hc_made, HC * u)
                    for w_sb, tile, full in ((w1_sb, gate, gate_full), (w2_sb, up, up_full)):
                        for k in range(DC):
                            i = pe.matmul(tile[:], w_sb[:, k, o * P:(o + 1) * P], yT[:, k, :],
                                          start=(k == 0), stop=(k == DC - 1))
                        i.then_inc(full, 1)

            def middle_layer(u, w_sb, loaded, src, src_made, out_taken, full):
                pe.wait_ge(src_made, HC * (u + 1))
                pe.wait_ge(loaded, 16)
                for o in range(HC):
                    if o >= 4:
                        pe.wait_ge(out_taken, HC * u + o - 4 + 1)
                    for k in range(HC):
                        i = pe.matmul(pm[o % 4][:], w_sb[:, k, o * P:(o + 1) * P], src[:, k, :],
                                      start=(k == 0), stop=(k == HC - 1))
                    i.then_inc(full, 1)

            def last_layer(u):
                pe.wait_ge(hc_made, HC * (u + 1))
                pe.wait_ge(w3_loaded, 16)
                if past(u):
                    pe.wait_ge(o_scaled, 2 * u)
                for half in range(2):
                    for t in range(2):
                        tok = (2 * half + t) * P
                        for k in range(HC):
                            i = pe.matmul(po[half][:, t * DIM:(t + 1) * DIM], hc[:, k, tok:tok + P], w3_sb[:, k, :],
                                          start=(k == 0), stop=(k == HC - 1))
                    i.then_inc(o_full, 1)

            def unit(u, last=False):
                gated_layers(u)
                middle_layer(u, h1_sb, h1_loaded, ha, ha_made, hb_made, mid1_full)
                if not last:
                    transposes(u + 1)
                middle_layer(u, h2_sb, h2_loaded, hb, hb_made, hc_made, mid2_full)
                last_layer(u)

            pe.wait_ge(made, 2)
            transposes(0)
            with pe.Fori(0, units - 1) as u:
                unit(u)
            unit(units - 1, last=True)

        @block.scalar
        def _(act):
            def squares(u):
                act.wait_ge(r_loaded, 16 * (u + 1))
                if past(u):
                    act.wait_ge(yT_full, DC * u)
                    act.wait_ge(msq_made, 2 * u)
                for t in range(NT):
                    act.activation(y[:, t, :], r_in[:, t, :], ACT.Square,
                                   accum_out=sq[:, t:t + 1]).then_inc(sq_made, 1)

            def take_yT(u):
                if past(u):
                    act.wait_ge(up_full, HC * u)
                for c in range(DC):
                    act.wait_ge(yT_full, DC * u + c + 1)
                    act.activation(yT[:, c, :], pt[c][:], ACT.Copy).then_inc(yT_made, 1)

            def unit(u, last=False):
                if past(u):
                    act.wait_ge(mid1_full, HC * u)
                for o in range(HC):
                    act.wait_ge(gate_full, HC * u + o + 1)
                    act.activation(ha[:, o, :], pm[2 * o % 4][:], ACT.Silu,
                                   scale=sc_sb[:, GATE, o:o + 1]).then_inc(silu_made, 1)
                if not last:
                    squares(u + 1)
                if past(u):
                    act.wait_ge(mid2_full, HC * u)
                for o in range(HC):
                    act.wait_ge(mid1_full, HC * u + o + 1)
                    act.activation(hb[:, o, :], pm[o % 4][:], ACT.Gelu,
                                   scale=sc_sb[:, MID1, o:o + 1]).then_inc(hb_made, 1)
                if not last:
                    take_yT(u + 1)
                if past(u):
                    act.wait_ge(o_full, 2 * u)
                for o in range(HC):
                    act.wait_ge(mid2_full, HC * u + o + 1)
                    act.activation(hc[:, o, :], pm[o % 4][:], ACT.Gelu,
                                   scale=sc_sb[:, MID2, o:o + 1]).then_inc(hc_made, 1)

            act.dma_start(nf_sb[:], norm_f.rearrange("(a d) -> a d", a=1).to_broadcast([P, DIM])).then_inc(small_loaded, 16)
            act.dma_start(s3_sb[:], w3_scale.rearrange("(a d) -> a d", a=1).to_broadcast([P, DIM])).then_inc(small_loaded, 16)
            act.dma_start(sc_sb[:], scales).then_inc(small_loaded, 16)
            squares(0)
            take_yT(0)
            act.wait_ge(small_loaded, 48)
            with act.Fori(0, units - 1) as u:
                unit(u)
            unit(units - 1, last=True)

        @block.vector
        def _(dve):
            def moments(u, which, src):
                for t in range(NT):
                    dve.bn_stats(stats[which][:, t, :], src[:, t, :]).then_inc(stats_made[which], 1)
                dve.wait_ge(stats_made[which], NT * (u + 1))
                dve.tensor_copy(spare[:], s3_sb[:, 0:1])
                for t in range(NT):
                    dve.bn_aggr(mom[which][:, t, :], stats[which][:, t, :]).then_inc(mom_made[which], 1)
                dve.wait_ge(mom_made[which], NT * (u + 1))
                dve.tensor_scalar(var[which][:], mom[which][:, :, 1], EPS, None, ALU.add).then_inc(var_made[which], 1)

            def normalise(u, which, src, dst, done):
                dve.wait_ge(rstd_made[which], u + 1)
                for t in range(NT):
                    dve.tensor_scalar(dst[:, t, :], src[:, t, :], mom[which][:, t, 0:1], rstd[which][:, t:t + 1],
                                      ALU.subtract, ALU.mult).then_inc(done, 1)

            def prepare(u):
                dve.wait_ge(rms_made, u + 1)
                for t in range(NT):
                    dve.scalar_tensor_tensor(out=r_in[:, t, :], in0=r_in[:, t, :], scalar=rms[:, t:t + 1],
                                             in1=nf_sb[:], op0=ALU.mult, op1=ALU.mult).then_inc(att_scaled, 1)
                dve.wait_ge(att_scaled, NT * (u + 1))
                moments(u, LN_ATT, r_in)
                normalise(u, LN_ATT, r_in, r_in, att_normed)
                dve.wait_ge(att_normed, NT * (u + 1))
                dve.wait_ge(x_loaded, 16 * (u + 1))
                dve.tensor_tensor(x1_next[:], x_in[:], r_in[:], ALU.add).then_inc(x1_made, 1)
                dve.wait_ge(x1_made, u + 1)
                moments(u, LN_IN, x1_next)
                normalise(u, LN_IN, x1_next, y, y_made)

            def gated(u):
                for o in range(HC):
                    dve.wait_ge(silu_made, HC * u + o + 1)
                    dve.wait_ge(up_full, HC * u + o + 1)
                    dve.scalar_tensor_tensor(out=ha[:, o, :], in0=pm[(2 * o + 1) % 4][:],
                                             scalar=sc_sb[:, UP, o:o + 1], in1=ha[:, o, :],
                                             op0=ALU.mult, op1=ALU.mult).then_inc(ha_made, 1)

            def close(u):
                if past(u):
                    dve.wait_ge(out_stored, 16 * u)
                for half in range(2):
                    dve.wait_ge(o_full, 2 * u + half + 1)
                    dve.tensor_tensor(o_sb[:, 2 * half:2 * half + 2, :],
                                      po[half][:].rearrange("p (t d) -> p t d", d=DIM),
                                      s3_sb[:].rearrange("p (a d) -> p a d", a=1).to_broadcast([P, 2, DIM]),
                                      ALU.mult).then_inc(o_scaled, 1)
                dve.wait_ge(o_scaled, 2 * (u + 1))
                moments(u, LN_OUT, o_sb)
                normalise(u, LN_OUT, o_sb, o_sb, o_normed)
                dve.wait_ge(o_normed, NT * (u + 1))
                dve.tensor_tensor(o_sb[:], o_sb[:], x1[:], ALU.add).then_inc(o_made, 1)

            def move_x1(u):
                if past(u):
                    dve.wait_ge(o_made, u)
                dve.tensor_copy(x1[:], x1_next[:]).then_inc(x1_moved, 1)
                dve.wait_ge(x1_moved, u + 1)

            def unit(u, first=False, last=False):
                gated(u)
                if not first:
                    close(u - 1)
                move_x1(u)
                if not last:
                    prepare(u + 1)

            dve.wait_ge(small_loaded, 48)
            prepare(0)
            unit(0, first=True)
            with dve.Fori(1, units - 1) as u:
                unit(u)
            unit(units - 1, last=True)
            close(units - 1)

        @block.gpsimd
        def _(pool):
            def root(u, which):
                pool.wait_ge(var_made[which], u + 1)
                pool.tensor_tensor(rstd[which][:], var[which][:], neg_half[:], ALU.pow).then_inc(rstd_made[which], 1)

            def root_mean_square(u):
                pool.wait_ge(sq_made, NT * (u + 1))
                if past(u):
                    pool.wait_ge(rms_made, u)
                    pool.wait_ge(att_scaled, NT * u)
                pool.tensor_tensor(msq[:], sq[:], per_dim[:], ALU.mult).then_inc(msq_made, 1)
                pool.wait_ge(msq_made, 2 * u + 1)
                pool.tensor_tensor(msq[:], msq[:], eps[:], ALU.add).then_inc(msq_made, 1)
                pool.wait_ge(msq_made, 2 * u + 2)
                pool.tensor_tensor(rms[:], msq[:], neg_half[:], ALU.pow).then_inc(rms_made, 1)

            def unit(u, first=False, last=False):
                if not first:
                    root(u - 1, LN_OUT)
                if not last:
                    root_mean_square(u + 1)
                    root(u + 1, LN_ATT)
                    root(u + 1, LN_IN)

            make_identity(pool, ident, made)
            for tile, value in ((neg_half, -0.5), (eps, EPS), (per_dim, 1.0 / DIM)):
                pool.memset(tile[:], value).then_inc(made, 1)
            pool.wait_ge(made, 5)
            root_mean_square(0)
            root(0, LN_ATT)
            root(0, LN_IN)
            unit(0, first=True)
            with pool.Fori(1, units - 1) as u:
                unit(u)
            unit(units - 1, last=True)
            root(units - 1, LN_OUT)


def build(nc, x, w_in, w_x, w_dt, w_out, vectors, a_log, norm_f, w1, w2, h1, h2, w3, scales, w3_scale, out):
    residual = nc.dram_tensor("residual", [SLOTS * LENGTH, DIM], F32).ap()
    normalise_input(nc, x, residual)
    mamba_layers(nc, residual, w_in, w_x, w_dt, w_out, vectors, a_log)
    feed_forward(nc, x, residual, norm_f, w1, w2, h1, h2, w3, scales, w3_scale, out)


def by_partition(np, a):
    layers, channels = a.shape[:2]
    return a.reshape(layers, channels // P, P, -1).transpose(0, 2, 1, 3).reshape(layers, P, -1)


def kernel(**inputs):
    import numpy as np
    import concourse.bacc as bacc
    from concourse.bass_utils import run_bass_kernel_spmd

    a = {k.replace("L0_attn_", "").replace("L0_ffn_", ""): np.asarray(v) for k, v in inputs.items()}
    arrays = {
        "x": a["hidden_states"].reshape(BATCH * LENGTH, DIM),
        "w_in": a["in_proj_w"].transpose(0, 2, 1),
        "w_x": a["x_proj_w"].transpose(0, 2, 1),
        "w_dt": a["dt_proj_w"].transpose(0, 2, 1),
        "w_out": a["out_proj_w"].transpose(0, 2, 1),
        "vectors": np.concatenate([by_partition(np, a[k]) for k in
                                   ("norm_w", "conv_w", "conv_b", "dt_proj_b", "D_param")], axis=2),
        "a_log": by_partition(np, a["A_log"]),
        "norm_f": a["norm_f_w"],
        "w1": a["w1_w"].T, "w2": a["w2_w"].T, "h1": a["h1_w"].T, "h2": a["h2_w"].T, "w3": a["w3_w"].T,
        "scales": np.stack([a[k].reshape(HC, P).T for k in ("w1_s", "w2_s", "h1_s", "h2_s")], axis=1),
        "w3_scale": a["w3_s"],
    }
    arrays = {k: np.ascontiguousarray(v) for k, v in arrays.items()}
    nc = bacc.Bacc("TRN2", target_bir_lowering=False, num_devices=1)
    aps = {k: nc.dram_tensor(f"{k}_dram", v.shape, F32, kind="ExternalInput").ap() for k, v in arrays.items()}
    out = nc.dram_tensor("out_dram", (BATCH * LENGTH, DIM), F32, kind="ExternalOutput").ap()
    build(nc, out=out, **aps)
    r = run_bass_kernel_spmd(nc, [{f"{k}_dram": v for k, v in arrays.items()}], core_ids=[0])
    return r.results[0]["out_dram"].reshape(BATCH, LENGTH, DIM)
```

```python
from contextlib import ExitStack

import concourse.bass as bass
from concourse import mybir

ALU = mybir.AluOpType
ACT = mybir.ActivationFunctionType
F32 = mybir.dt.float32
F32R = mybir.dt.float32r
I32 = mybir.dt.int32

P = 128
BATCH, LENGTH, DIM = 4, 1024, 256
LAYERS, STATES, TAPS = 4, 16, 4
INNER = 2 * DIM
RANK = DIM // 16
HIDDEN = 1024
EPS = 1e-5

TOK = 512
NT = TOK // P
DC = DIM // P
EC = INNER // P
HC = HIDDEN // P
HALVES = LENGTH // TOK
GROUP = 4
NG = STATES // GROUP
STEPS = NG * EC
XD = RANK + 2 * STATES

PAIR = 2
ROUNDS = BATCH * LAYERS
PER_PAIR = PAIR * LAYERS
SLOTS = ROUNDS + (BATCH // PAIR) * PAIR

V_NORM = 0
V_CONV = V_NORM + DC
V_CBIAS = V_CONV + EC * TAPS
V_DTBIAS = V_CBIAS + EC
V_SKIP = V_DTBIAS + EC
V_ALL = V_SKIP + EC


def past(count):
    return not isinstance(count, int) or count > 0


def slot_of(rnd):
    return rnd + PAIR * (rnd // PER_PAIR)


def layer_of(rnd):
    return (rnd % PER_PAIR) // PAIR


def rows(slot, half):
    return bass.ds(slot * LENGTH + half * TOK, TOK)


def tokens_view(dram_rows):
    return dram_rows.rearrange("(t p) d -> p t d", p=P)


def make_identity(pool, ident, made):
    pool.memset(ident[:], 0.0).then_inc(made, 1)
    pool.wait_ge(made, 1)
    pool.affine_select(out=ident[:], in_=ident[:], compare_op=ALU.not_equal, fill=1.0, base=0,
                       pattern=[[-1, P]], channel_multiplier=1).then_inc(made, 1)


def normalise_input(nc, x, residual, weights, exact):
    units = BATCH * HALVES
    cols = DC * HIDDEN
    chunks = []
    for w in weights:
        rows_of_chunk = cols * P // w.shape[1]
        chunks += [w[r:r + rows_of_chunk, :].rearrange("(c p) o -> p c o", p=P)
                   for r in range(0, w.shape[0], rows_of_chunk)]
    RING = 3
    with ExitStack() as ctx:
        def sb(name, shape):
            return ctx.enter_context(nc.sbuf_tensor(name, shape, F32))

        def sem(name):
            return ctx.enter_context(nc.semaphore(name))

        xin = [sb(f"pre_x{h}", [P, NT, DIM]) for h in range(2)]
        yout = [sb(f"pre_y{h}", [P, NT, DIM]) for h in range(2)]
        stats = [sb(f"pre_stats{h}", [P, NT, 6]) for h in range(2)]
        moments = [sb(f"pre_moments{h}", [P, NT, 2]) for h in range(2)]
        var = [sb(f"pre_var{h}", [P, NT]) for h in range(2)]
        root = [sb(f"pre_root{h}", [P, NT]) for h in range(2)]
        rstd = [sb(f"pre_rstd{h}", [P, NT]) for h in range(2)]
        wt = [sb(f"pre_wt{i}", [P, cols]) for i in range(RING)]
        rounded = [ctx.enter_context(nc.sbuf_tensor(f"pre_rounded{i}", [P, cols], F32R)) for i in range(2)]
        lost = sb("pre_lost", [P, len(chunks)])
        lost_sum = sb("pre_lost_sum", [P, 1])
        ones = sb("pre_ones", [P, 1])
        exact_sb = ctx.enter_context(nc.sbuf_tensor("pre_exact", [1, 1], I32))
        lost_all = ctx.enter_context(nc.psum_tensor("pre_lost_all", [P, TOK], F32))

        loaded = [sem(f"pre_loaded{h}") for h in range(2)]
        stored = [sem(f"pre_stored{h}") for h in range(2)]
        stats_done = sem("pre_stats_done")
        moments_done = sem("pre_moments_done")
        var_done = sem("pre_var_done")
        root_done = sem("pre_root_done")
        rstd_done = sem("pre_rstd_done")
        y_done = sem("pre_y_done")
        wt_loaded = [sem(f"pre_wt_loaded{i}") for i in range(RING)]
        rounded_made, diff_made, lost_made = sem("pre_rounded_made"), sem("pre_diff_made"), sem("pre_lost_made")
        ones_made, lost_all_made = sem("pre_ones_made"), sem("pre_lost_all_made")
        exact_made, exact_stored = sem("pre_exact_made"), sem("pre_exact_stored")

        block = ctx.enter_context(nc.Block())

        @block.sync
        def _(sp):
            for u in range(units):
                h = u % 2
                if u >= 2:
                    sp.wait_ge(y_done, NT * (u - 1))
                sp.dma_start(xin[h][:], tokens_view(x[bass.ds(u * TOK, TOK), :])).then_inc(loaded[h], 16)
            sp.wait_ge(exact_made, 1)
            sp.dma_start(exact, exact_sb[:]).then_inc(exact_stored, 16)
            sp.wait_ge(exact_stored, 16)

        @block.tensor
        def _(pe):
            pe.wait_ge(ones_made, 1)
            pe.wait_ge(lost_made, len(chunks) + 1)
            pe.matmul(lost_all[0:1, 0:1], lost_sum[:], ones[:], start=True, stop=True).then_inc(lost_all_made, 1)

        @block.gpsimd
        def _(pool):
            def differ(i):
                pool.wait_ge(rounded_made, i + 1)
                pool.tensor_tensor(wt[i % RING][:], wt[i % RING][:], rounded[i % 2][:],
                                   ALU.subtract).then_inc(diff_made, 1)

            def store(u):
                h = u % 2
                seq, half = u // HALVES, u % HALVES
                slot = slot_of(PER_PAIR * (seq // PAIR) + seq % PAIR)
                pool.wait_ge(y_done, NT * (u + 1))
                pool.dma_start(tokens_view(residual[rows(slot, half), :]), yout[h][:]).then_inc(stored[h], 16)
            for i in range(len(chunks)):
                if 2 <= i < units + 2:
                    store(i - 2)
                differ(i)
            for h in range(2):
                pool.wait_ge(stored[h], 16 * (units // 2))

        @block.scalar
        def _(act):
            def load_chunk(i):
                if i >= RING:
                    act.wait_ge(lost_made, i - RING + 1)
                act.dma_start(wt[i % RING][:].rearrange("p (c o) -> p c o", o=chunks[i].shape[2]),
                              chunks[i]).then_inc(wt_loaded[i % RING], 16)

            def add_up(i):
                act.wait_ge(diff_made, i + 1)
                act.activation(wt[i % RING][:], wt[i % RING][:], ACT.Abs,
                               accum_out=lost[:, i:i + 1]).then_inc(lost_made, 1)

            for i in range(RING):
                load_chunk(i)
            for i in range(len(chunks)):
                if i < units:
                    h = i % 2
                    act.wait_ge(var_done, i + 1)
                    act.activation(root[h][:], var[h][:], ACT.Sqrt).then_inc(root_done, 1)
                act.wait_ge(wt_loaded[i % RING], 16 * (i // RING + 1))
                if i >= 2:
                    act.wait_ge(diff_made, i - 1)
                act.activation(rounded[i % 2][:], wt[i % RING][:], ACT.Copy).then_inc(rounded_made, 1)
                if i >= 1:
                    add_up(i - 1)
                    if i - 1 + RING < len(chunks):
                        load_chunk(i - 1 + RING)
            add_up(len(chunks) - 1)
            act.wait_ge(lost_made, len(chunks))
            act.activation(lost[:], lost[:], ACT.Copy, accum_out=lost_sum[:]).then_inc(lost_made, 1)

        @block.vector
        def _(dve):
            dve.memset(ones[:], 1.0).then_inc(ones_made, 1)
            for u in range(units):
                h = u % 2
                dve.wait_ge(loaded[h], 16 * (u // 2 + 1))
                for t in range(NT):
                    dve.bn_stats(stats[h][:, t, :], xin[h][:, t, :]).then_inc(stats_done, 1)
                for t in range(NT):
                    dve.wait_ge(stats_done, NT * u + t + 1)
                    dve.bn_aggr(moments[h][:, t, :], stats[h][:, t, :]).then_inc(moments_done, 1)
                dve.wait_ge(moments_done, NT * (u + 1))
                if u >= 2:
                    dve.wait_ge(root_done, u - 1)
                dve.tensor_scalar(var[h][:], moments[h][:, :, 1], EPS, None, ALU.add).then_inc(var_done, 1)
                dve.wait_ge(root_done, u + 1)
                dve.reciprocal(rstd[h][:], root[h][:]).then_inc(rstd_done, 1)
                dve.wait_ge(rstd_done, u + 1)
                if u >= 2:
                    dve.wait_ge(stored[h], 16 * (u // 2))
                for t in range(NT):
                    dve.tensor_scalar(yout[h][:, t, :], xin[h][:, t, :], moments[h][:, t, 0:1],
                                      rstd[h][:, t:t + 1], ALU.subtract, ALU.mult).then_inc(y_done, 1)
            dve.wait_ge(lost_all_made, 1)
            dve.tensor_scalar(exact_sb[:], lost_all[0:1, 0:1], 0.0, None, ALU.is_equal).then_inc(exact_made, 1)


def mamba_layers(nc, residual, w_in, w_x, w_dt, w_out, vectors, a_log):
    with ExitStack() as ctx:
        def sb(name, shape):
            return ctx.enter_context(nc.sbuf_tensor(name, shape, F32))

        def sem(name):
            return ctx.enter_context(nc.semaphore(name))

        ident = sb("ident", [P, P])
        win = sb("win", [P, DC, 2 * INNER])
        wx = sb("wx", [P, EC, XD])
        wdt = sb("wdt", [RANK, INNER])
        wout = sb("wout", [P, EC, DIM])
        vec = sb("vec", [P, V_ALL])
        alog = sb("alog", [P, EC * STATES])
        aexp = sb("aexp", [P, EC * STATES])
        aneg = sb("aneg", [P, EC * STATES])
        r_a = sb("r_a", [P, NT, DIM])
        hnT = sb("hnT", [P, DC, TOK])
        neg_half, eps, per_dim = sb("neg_half", [P, NT]), sb("eps", [P, NT]), sb("per_dim", [P, NT])
        zeros = sb("zeros", [P, EC, TAPS - 1])
        ln_one = sb("ln_one", [P, 1])
        sq = sb("sq", [P, NT])
        msq = sb("msq", [P, NT])
        rs = sb("rs", [P, NT])
        xi = sb("xi", [P, EC, TAPS - 1 + TOK])
        cv = sb("cv", [P, EC, TOK])
        uu = sb("uu", [P, EC, TOK])
        skip = sb("skip", [P, EC, TOK])
        dt = [sb(f"dt{h}", [P, EC, TOK]) for h in range(2)]
        dtu = [sb(f"dtu{h}", [P, EC, TOK]) for h in range(2)]
        gate = [sb(f"gate{h}", [P, NT, INNER]) for h in range(2)]
        xdb = [sb(f"xdb{h}", [P, NT, XD]) for h in range(2)]
        dtin = sb("dtin", [RANK, TOK])
        b_all = [sb(f"b_all{i}", [P, GROUP, TOK]) for i in range(2)]
        c_all = [sb(f"c_all{i}", [P, GROUP, TOK]) for i in range(2)]
        decay = [sb(f"decay{i}", [P, GROUP, TOK]) for i in range(2)]
        hx = [sb(f"hx{c}", [P, GROUP, TOK]) for c in range(EC)]
        hlast = sb("hlast", [P, EC * STATES])
        yg = [sb(f"yg{i}", [P, NT, P]) for i in range(2)]
        ygT = sb("ygT", [P, EC, TOK])
        r_c = sb("r_c", [P, NT, DIM])

        ysum = [ctx.enter_context(nc.psum_tensor(f"ysum{c}", [P, TOK], F32)) for c in range(EC)]
        pq = [ctx.enter_context(nc.psum_tensor(f"pq{i}", [P, TOK], F32)) for i in range(2)]
        pp = [ctx.enter_context(nc.psum_tensor(f"pp{i}", [P, TOK], F32)) for i in range(2)]

        ident_made, ln_one_made = sem("ident_made"), sem("ln_one_made")
        win_loaded, wx_loaded, wout_loaded = sem("win_loaded"), sem("wx_loaded"), sem("wout_loaded")
        vec_loaded, alog_loaded = sem("vec_loaded"), sem("alog_loaded")
        ra_loaded, rc_loaded, r_stored = sem("ra_loaded"), sem("rc_loaded"), sem("r_stored")
        hnT_full, xi_full, z_full, xdb_full = sem("hnT_full"), sem("xi_full"), sem("z_full"), sem("xdb_full")
        dtin_full, dt_full, bc_full = sem("dtin_full"), sem("dt_full"), sem("bc_full")
        ysum_done, back_full, out_full = sem("ysum_done"), sem("back_full"), sem("out_full")
        aneg_made, sq_made = sem("aneg_made"), sem("sq_made")
        hnT_made, xi_made, u_made, gate_made = sem("hnT_made"), sem("xi_made"), sem("u_made"), sem("gate_made")
        xdb_made, dtin_made, xb_made = sem("xdb_made"), sem("dtin_made"), sem("xb_made")
        abs_made, e_made, ln_made, skip_made = sem("abs_made"), sem("e_made"), sem("ln_made"), sem("skip_made")
        decay_made, b_made, c_made, ygT_made = sem("decay_made"), sem("b_made"), sem("c_made"), sem("ygT_made")
        scan_done, hlast_saved, hc_made = sem("scan_done"), sem("hlast_saved"), sem("hc_made")
        conv_done, rest_steps, rest_made = sem("conv_done"), sem("rest_steps"), sem("rest_made")
        dt_made = sem("dt_made")
        yg_made, r_made = sem("yg_made"), sem("r_made")
        rs_made, hn_made, lead_made = sem("rs_made"), sem("hn_made"), sem("lead_made")
        dtu_made, inject_made = sem("dtu_made"), sem("inject_made")

        block = ctx.enter_context(nc.Block())


        @block.sync
        def _(sp):
            def load_prep_weights(j):
                v = 2 * j - 1
                lay = layer_of(j)
                if past(v):
                    sp.wait_ge(z_full, 4 * (v + 1))
                sp.dma_start(win[:], w_in[lay].rearrange("(c p) e -> p c e", p=P)).then_inc(win_loaded, 16)
                if past(v):
                    sp.wait_ge(dt_full, 4 * (v + 1))
                sp.dma_start(wx[:], w_x[lay].rearrange("(c p) r -> p c r", p=P)).then_inc(wx_loaded, 16)
                sp.dma_start(wdt[:], w_dt[lay]).then_inc(wx_loaded, 16)
                if past(v):
                    sp.wait_ge(skip_made, EC * (v + 1))
                sp.dma_start(vec[:], vectors[lay]).then_inc(vec_loaded, 16)

            def load_alog(j):
                if past(j):
                    sp.wait_ge(aneg_made, 2 * (j - 1) + 1)
                sp.dma_start(alog[:], a_log[layer_of(j)]).then_inc(alog_loaded, 16)

            def load_ra(j, h):
                v = 2 * j + h
                if past(v):
                    sp.wait_ge(hnT_full, DC * v)
                if past(v - 3):
                    sp.wait_ge(r_stored, 16 * (v - 3))
                sp.dma_start(r_a[:], tokens_view(residual[rows(slot_of(j), h), :])).then_inc(ra_loaded, 16)

            def load_rc(j, h):
                w = 2 * j + h
                if past(w):
                    sp.wait_ge(r_stored, 16 * w)
                sp.dma_start(r_c[:], tokens_view(residual[rows(slot_of(j), h), :])).then_inc(rc_loaded, 16)

            def store(j, h):
                w = 2 * j + h
                sp.wait_ge(r_made, 2 * (w + 1))
                sp.dma_start(tokens_view(residual[rows(slot_of(j) + PAIR, h), :]), r_c[:]).then_inc(r_stored, 16)

            def stage(j, h, first=False, last=False):
                u = 2 * j + h
                if not first:
                    load_rc(j + h - 1, 1 - h)
                if not last:
                    load_ra(j + h, 1 - h)
                if h == 1 and not last:
                    load_alog(j + 1)
                if not first:
                    store(j + h - 1, 1 - h)
                if h == 0:
                    if not first:
                        sp.wait_ge(out_full, 2 * u)
                    sp.dma_start(wout[:], w_out[layer_of(j)].rearrange("(c p) d -> p c d", p=P)).then_inc(wout_loaded, 16)
                    if not isinstance(j, int) or j + 1 < ROUNDS:
                        load_prep_weights(j + 1)

            load_prep_weights(0)
            load_alog(0)
            load_ra(0, 0)
            stage(0, 0, first=True)
            stage(0, 1)
            with sp.Fori(1, ROUNDS - 1) as j:
                stage(j, 0)
                stage(j, 1)
            stage(ROUNDS - 1, 0)
            stage(ROUNDS - 1, 1, last=True)
            load_rc(ROUNDS - 1, 1)
            store(ROUNDS - 1, 1)
            sp.wait_ge(r_stored, 16 * 2 * ROUNDS)

        @block.tensor
        def _(pe):
            def norm_transposes(j, h):
                v = 2 * j + h
                pe.wait_ge(hn_made, v + 1)
                for c in range(DC):
                    if past(v - 1):
                        pe.wait_ge(r_made, 2 * (v - 2) + c + 1)
                    elif past(v):
                        pe.wait_ge(xb_made, EC * (v - 1) + 2 + c + 1)
                    for t in range(NT):
                        i = pe.transpose(pp[c][:, t * P:(t + 1) * P], r_a[:, t, c * P:(c + 1) * P], ident[:])
                    i.then_inc(hnT_full, 1)

            def in_projection_x(j, h, tiles):
                v = 2 * j + h
                pe.wait_ge(hnT_made, DC * (v + 1))
                pe.wait_ge(win_loaded, 16 * (j + 1))
                for c in tiles:
                    if c >= 2:
                        pe.wait_ge(xi_made, 2 * (EC * v + c - 2 + 1))
                    for k in range(DC):
                        i = pe.matmul(pp[c % 2][:], win[:, k, c * P:(c + 1) * P], hnT[:, k, :],
                                      start=(k == 0), stop=(k == DC - 1))
                    i.then_inc(xi_full, 1)

            def in_projection_z(j, h, tiles):
                v = 2 * j + h
                for t in tiles:
                    if t < 2:
                        pe.wait_ge(xi_made, 2 * (EC * v + t + 2 + 1))
                    else:
                        pe.wait_ge(gate_made, NT * v + t - 2 + 1)
                    for k in range(DC):
                        i = pe.matmul(pp[t % 2][:], hnT[:, k, t * P:(t + 1) * P], win[:, k, INNER:2 * INNER],
                                      start=(k == 0), stop=(k == DC - 1))
                    i.then_inc(z_full, 1)

            def x_projection(j, h):
                v = 2 * j + h
                pe.wait_ge(u_made, v + 1)
                pe.wait_ge(wx_loaded, 32 * (j + 1))
                pe.wait_ge(gate_made, NT * v + 3)
                for t in range(NT):
                    for c in range(EC):
                        i = pe.matmul(pp[0][:, t * XD:(t + 1) * XD], uu[:, c, t * P:(t + 1) * P], wx[:, c, :],
                                      start=(c == 0), stop=(c == EC - 1))
                i.then_inc(xdb_full, 1)

            def dt_transposes(j, h):
                v = 2 * j + h
                pe.wait_ge(xdb_made, v + 1)
                pe.wait_ge(gate_made, NT * v + 4)
                for t in range(NT):
                    i = pe.transpose(pp[1][0:RANK, t * P:(t + 1) * P], xdb[h][:, t, 0:RANK], ident[:])
                i.then_inc(dtin_full, 1)

            def dt_projection(j, h):
                v = 2 * j + h
                pe.wait_ge(dtin_made, v + 1)
                for c in range(EC):
                    if c >= 2:
                        pe.wait_ge(xb_made, EC * v + c - 2 + 1)
                    pe.matmul(pp[c % 2][:], wdt[:, c * P:(c + 1) * P], dtin[:], start=True,
                              stop=True).then_inc(dt_full, 1)

            def spread(v, h, g, i):
                n = i % GROUP
                col = RANK + (STATES if i >= GROUP else 0) + GROUP * g + n
                if i < 2:
                    if past(STATES * v + GROUP * g):
                        pe.wait_ge(c_made, STATES * v + GROUP * g + i - 1)
                elif i < 2 + GROUP:
                    pe.wait_ge(b_made, STATES * v + GROUP * g + i - 2 + 1)
                else:
                    pe.wait_ge(c_made, STATES * v + GROUP * g + i - 2 - GROUP + 1)
                if g == 0 and i == 0:
                    pe.wait_ge(xdb_made, v + 1)
                for t in range(NT):
                    ins = pe.transpose(pq[i % 2][:, t * P:(t + 1) * P],
                                       xdb[h][:, t, col:col + 1].to_broadcast([P, P]), ident[:])
                ins.then_inc(bc_full, 1)

            def sum_states(u, k):
                g, c = k // EC, k % EC
                if g == 0:
                    if past(u):
                        pe.wait_ge(yg_made, EC * (u - 1) + c + 1)
                    pe.wait_ge(skip_made, EC * (u + 1))
                    for t in range(NT):
                        pe.matmul(ysum[c][:, t * P:(t + 1) * P], skip[:, c, t * P:(t + 1) * P], ident[:],
                                  is_transpose=True, start=(t == 0), stop=False, skip_group_check=True)
                pe.wait_ge(hc_made, STEPS * u + k + 1)
                for n in range(GROUP):
                    for t in range(NT):
                        i = pe.matmul(ysum[c][:, t * P:(t + 1) * P], hx[c][:, n, t * P:(t + 1) * P], ident[:],
                                      is_transpose=True, start=False, stop=(g == NG - 1 and n == GROUP - 1),
                                      skip_group_check=True)
                i.then_inc(ysum_done, 1)

            def back_transposes(w, c, last=False):
                pe.wait_ge(yg_made, EC * w + c + 1)
                if c >= 2:
                    pe.wait_ge(ygT_made, EC * w + c - 2 + 1)
                elif last:
                    pe.wait_ge(r_made, 2 * (w - 1) + c + 1)
                else:
                    pe.wait_ge(xb_made, EC * (w + 1) + 2 + c + 1)
                for t in range(NT):
                    i = pe.transpose(pp[c % 2][:, t * P:(t + 1) * P], yg[c % 2][:, t, :], ident[:])
                i.then_inc(back_full, 1)

            def out_projection(j, h):
                w = 2 * j + h
                pe.wait_ge(ygT_made, EC * (w + 1))
                pe.wait_ge(wout_loaded, 16 * (j + 1))
                for i2 in range(2):
                    for t in range(2):
                        for c in range(EC):
                            tok = (2 * i2 + t) * P
                            i = pe.matmul(pp[i2][:, t * DIM:(t + 1) * DIM], ygT[:, c, tok:tok + P], wout[:, c, :],
                                          start=(c == 0), stop=(c == EC - 1))
                    i.then_inc(out_full, 1)

            def stage(j, h, first=False, last=False):
                u = 2 * j + h
                jv, hv = j + h, 1 - h
                jw, hw = j + h - 1, 1 - h
                for k in range(STEPS):
                    g = k // EC
                    for i in range(2 * (k % EC), 2 * (k % EC) + 2):
                        if g < NG - 1:
                            spread(u, h, g + 1, i)
                        elif not last:
                            spread(u + 1, hv, 0, i)
                    if k < 3 and not first:
                        back_transposes(u - 1, k + 1, last)
                    if k == 3 and not first:
                        out_projection(jw, hw)
                    if not last:
                        if k == 4:
                            norm_transposes(jv, hv)
                        if k == 5:
                            in_projection_x(jv, hv, (0, 1))
                        if k == 6:
                            in_projection_x(jv, hv, (2, 3))
                        if k == 7:
                            in_projection_z(jv, hv, (0, 1))
                        if k == 8:
                            in_projection_z(jv, hv, (2, 3))
                        if k == 9:
                            x_projection(jv, hv)
                        if k == 10:
                            dt_transposes(jv, hv)
                        if k == 11:
                            dt_projection(jv, hv)
                    if k == 15:
                        back_transposes(u, 0, last)
                    if k > 0:
                        sum_states(u, k - 1)
                    elif not first:
                        sum_states(u - 1, STEPS - 1)

            pe.wait_ge(ident_made, 2)
            norm_transposes(0, 0)
            in_projection_x(0, 0, range(EC))
            in_projection_z(0, 0, range(NT))
            x_projection(0, 0)
            dt_transposes(0, 0)
            dt_projection(0, 0)
            for i in range(2 * GROUP):
                spread(0, 0, 0, i)
            stage(0, 0, first=True)
            stage(0, 1)
            with pe.Fori(1, ROUNDS - 1) as j:
                stage(j, 0)
                stage(j, 1)
            stage(ROUNDS - 1, 0)
            stage(ROUNDS - 1, 1, last=True)
            sum_states(2 * ROUNDS - 1, STEPS - 1)
            for c in range(1, EC):
                back_transposes(2 * ROUNDS - 1, c, last=True)
            out_projection(ROUNDS - 1, 1)

        @block.scalar
        def _(act):
            def square_sums(j, h):
                v = 2 * j + h
                act.wait_ge(ra_loaded, 16 * (v + 1))
                if past(v):
                    act.wait_ge(z_full, NT * v)
                    act.wait_ge(rs_made, 3 * v)
                for t in range(NT):
                    act.activation(hnT[:, t // 2, t % 2 * DIM:(t % 2 + 1) * DIM], r_a[:, t, :], ACT.Square,
                                   accum_out=sq[:, t:t + 1]).then_inc(sq_made, 1)

            def take_hnT(j, h):
                v = 2 * j + h
                act.wait_ge(vec_loaded, 16 * (j + 1))
                if past(v):
                    act.wait_ge(z_full, NT * v)
                for c in range(DC):
                    act.wait_ge(hnT_full, DC * v + c + 1)
                    act.activation(hnT[:, c, :], pp[c][:], ACT.Copy,
                                   scale=vec[:, V_NORM + c:V_NORM + c + 1]).then_inc(hnT_made, 1)

            def take_xi(j, h, tiles):
                v = 2 * j + h
                act.wait_ge(lead_made, v + 1)
                if past(v):
                    act.wait_ge(rest_made, v)
                for c in tiles:
                    act.wait_ge(xi_full, EC * v + c + 1)
                    act.activation(xi[:, c, TAPS - 1:], pp[c % 2][:], ACT.Copy).then_inc(xi_made, 1)
                    tap = V_CONV + c * TAPS + TAPS - 1
                    act.activation(cv[:, c, :], pp[c % 2][:], ACT.Identity, scale=vec[:, tap:tap + 1],
                                   bias=vec[:, V_CBIAS + c:V_CBIAS + c + 1]).then_inc(xi_made, 1)

            def silus(j, h):
                v = 2 * j + h
                if past(v - 1):
                    act.wait_ge(yg_made, EC * (v - 1))
                for t in range(NT):
                    act.wait_ge(z_full, NT * v + t + 1)
                    act.activation(gate[h][:, t, :], pp[t % 2][:], ACT.Silu).then_inc(gate_made, 1)
                act.wait_ge(conv_done, EC * (TAPS - 1) * (v + 1))
                if past(v):
                    act.wait_ge(dtu_made, EC * v)
                    act.wait_ge(skip_made, EC * v)
                    act.wait_ge(xdb_full, v)
                act.activation(uu[:], cv[:], ACT.Silu).then_inc(u_made, 1)
                act.preload_act_table_set("natural_log_exp_and_others")

            def take_xdb(j, h):
                v = 2 * j + h
                act.wait_ge(xdb_full, v + 1)
                if past(v - 1):
                    act.wait_ge(c_made, STATES * (v - 1))
                act.activation(xdb[h][:].rearrange("p t r -> p (t r)"), pp[0][:, 0:NT * XD],
                               ACT.Copy).then_inc(xdb_made, 1)

            def take_dtin(j, h):
                v = 2 * j + h
                act.wait_ge(dtin_full, v + 1)
                if past(v):
                    act.wait_ge(dt_full, EC * v)
                act.activation(dtin[:], pp[1][0:RANK, :], ACT.Copy).then_inc(dtin_made, 1)

            def take_dt(j, h):
                v = 2 * j + h
                act.wait_ge(u_made, v + 1)
                for c in range(EC):
                    act.wait_ge(dt_full, EC * v + c + 1)
                    act.activation(cv[:, c, :], pp[c % 2][:], ACT.Identity,
                                   bias=vec[:, V_DTBIAS + c:V_DTBIAS + c + 1]).then_inc(xb_made, 1)

            def softplus_exp(j, h):
                v = 2 * j + h
                act.wait_ge(xb_made, EC * (v + 1))
                if past(v - 1):
                    act.wait_ge(inject_made, STEPS * (v - 1))
                act.activation(dtu[h][:], cv[:], ACT.Abs).then_inc(abs_made, 1)
                act.wait_ge(abs_made, v + 1)
                act.activation(dtu[h][:], dtu[h][:], ACT.Exp, scale=-1.0).then_inc(e_made, 1)

            def softplus_ln(j, h):
                v = 2 * j + h
                act.wait_ge(e_made, v + 1)
                if past(v - 1):
                    act.wait_ge(decay_made, GROUP * STEPS * (v - 1))
                    act.wait_ge(dtu_made, EC * (v - 1))
                act.activation(dt[h][:], dtu[h][:], ACT.Ln, bias=1.0).then_inc(ln_made, 1)

            def skips(j, h):
                v = 2 * j + h
                act.wait_ge(dt_made, v + 1)
                act.wait_ge(u_made, v + 1)
                for c in range(EC):
                    act.activation(skip[:, c, :], uu[:, c, :], ACT.Copy,
                                   scale=vec[:, V_SKIP + c:V_SKIP + c + 1]).then_inc(skip_made, 1)

            def make_aneg(j):
                u = 2 * j
                act.wait_ge(alog_loaded, 16 * (j + 1))
                if past(u):
                    act.wait_ge(decay_made, GROUP * STEPS * u)
                act.activation(aexp[:], alog[:], ACT.Exp).then_inc(aneg_made, 1)
                act.wait_ge(aneg_made, 2 * j + 1)
                act.activation(aneg[:], aexp[:], ACT.Copy, scale=-1.0).then_inc(aneg_made, 1)
                act.wait_ge(aneg_made, 2 * j + 2)

            def decays(u, h, k):
                g, c = k // EC, k % EC
                if k == 0:
                    act.wait_ge(dt_made, u + 1)
                if past(STEPS * u + k - 1):
                    act.wait_ge(scan_done, STEPS * u + k - 1)
                for n in range(GROUP):
                    col = c * STATES + g * GROUP + n
                    act.activation(decay[k % 2][:, n, :], dt[h][:, c, :], ACT.Exp,
                                   scale=aneg[:, col:col + 1]).then_inc(decay_made, 1)

            def take_spread(v, g, i):
                act.wait_ge(bc_full, 2 * STATES * v + 2 * GROUP * g + i + 1)
                n = i % GROUP
                done = STEPS * v + EC * (g - 1)
                if i < GROUP:
                    if past(done):
                        act.wait_ge(inject_made, done)
                    act.activation(b_all[g % 2][:, n, :], pq[i % 2][:], ACT.Copy).then_inc(b_made, 1)
                else:
                    if past(done):
                        act.wait_ge(hc_made, done)
                    act.activation(c_all[g % 2][:, n, :], pq[i % 2][:], ACT.Copy).then_inc(c_made, 1)

            def take_back(w, c):
                act.wait_ge(back_full, EC * w + c + 1)
                if past(w):
                    act.wait_ge(out_full, 2 * w)
                act.activation(ygT[:, c, :], pp[c % 2][:], ACT.Copy).then_inc(ygT_made, 1)

            def stage(j, h, first=False, last=False):
                u = 2 * j + h
                jv, hv = j + h, 1 - h
                for k in range(STEPS):
                    g = k // EC
                    if k < STEPS - 1:
                        decays(u, h, k + 1)
                    elif not last:
                        if h == 1:
                            make_aneg(j + 1)
                        decays(u + 1, hv, 0)
                    for i in range(2 * (k % EC), 2 * (k % EC) + 2):
                        if g < NG - 1:
                            take_spread(u, g + 1, i)
                        elif not last:
                            take_spread(u + 1, 0, i)
                    if k < 3 and not first:
                        take_back(u - 1, k + 1)
                    if not last:
                        if k == 0:
                            square_sums(jv, hv)
                        if k == 4:
                            take_hnT(jv, hv)
                        if k == 5:
                            take_xi(jv, hv, (0, 1))
                        if k == 6:
                            take_xi(jv, hv, (2, 3))
                        if k == 8:
                            silus(jv, hv)
                        if k == 9:
                            take_xdb(jv, hv)
                        if k == 10:
                            take_dtin(jv, hv)
                        if k == 11:
                            take_dt(jv, hv)
                        if k == 12:
                            softplus_exp(jv, hv)
                        if k == 13:
                            softplus_ln(jv, hv)
                        if k == 15:
                            skips(jv, hv)
                    if k == 15:
                        take_back(u, 0)

            act.preload_act_table_set("natural_log_exp_and_others")
            act.wait_ge(ident_made, 6)
            act.activation(ln_one[:], zeros[:, 0, 0:1], ACT.Ln, bias=1.0).then_inc(ln_one_made, 1)
            square_sums(0, 0)
            take_hnT(0, 0)
            take_xi(0, 0, range(EC))
            silus(0, 0)
            take_xdb(0, 0)
            take_dtin(0, 0)
            take_dt(0, 0)
            softplus_exp(0, 0)
            softplus_ln(0, 0)
            skips(0, 0)
            for i in range(2 * GROUP):
                take_spread(0, 0, i)
            make_aneg(0)
            decays(0, 0, 0)
            stage(0, 0, first=True)
            stage(0, 1)
            with act.Fori(1, ROUNDS - 1) as j:
                stage(j, 0)
                stage(j, 1)
            stage(ROUNDS - 1, 0)
            stage(ROUNDS - 1, 1, last=True)
            for c in range(1, EC):
                take_back(2 * ROUNDS - 1, c)

        @block.vector
        def _(dve):
            def convolve(j, h, pair):
                v = 2 * j + h
                done = EC * (TAPS - 1) * v + 2 * (TAPS - 1) * pair
                for tap in range(TAPS - 1):
                    for c in (2 * pair, 2 * pair + 1):
                        if tap == 0:
                            dve.wait_ge(xi_made, 2 * (EC * v + c + 1))
                        else:
                            dve.wait_ge(conv_done, done + 2 * (tap - 1) + c - 2 * pair + 1)
                        col = V_CONV + c * TAPS + tap
                        dve.scalar_tensor_tensor(out=cv[:, c, :], in0=xi[:, c, tap:tap + TOK],
                                                 scalar=vec[:, col:col + 1], in1=cv[:, c, :],
                                                 op0=ALU.mult, op1=ALU.add).then_inc(conv_done, 1)

            def softplus_rest(j, h):
                v = 2 * j + h
                dve.wait_ge(e_made, v + 1)
                if past(v):
                    dve.wait_ge(ysum_done, STEPS * (v - 1) + EC)
                dve.tensor_scalar(skip[:], dtu[h][:], 1.0, None, ALU.add).then_inc(rest_steps, 1)
                dve.wait_ge(rest_steps, 2 * v + 1)
                dve.scalar_tensor_tensor(out=skip[:], in0=skip[:], scalar=1.0, in1=dtu[h][:],
                                         op0=ALU.subtract, op1=ALU.subtract).then_inc(rest_steps, 1)

            def softplus_linear(j, h):
                v = 2 * j + h
                dve.wait_ge(rest_steps, 2 * v + 2)
                dve.scalar_tensor_tensor(out=skip[:], in0=cv[:], scalar=0.0, in1=skip[:],
                                         op0=ALU.max, op1=ALU.subtract).then_inc(rest_made, 1)

            def softplus_sum(j, h):
                v = 2 * j + h
                dve.wait_ge(rest_made, v + 1)
                dve.wait_ge(ln_made, v + 1)
                dve.scalar_tensor_tensor(out=dt[h][:], in0=dt[h][:], scalar=ln_one[:, 0:1], in1=skip[:],
                                         op0=ALU.subtract, op1=ALU.add).then_inc(dt_made, 1)

            def recur(j, h, k):
                u = 2 * j + h
                g, c = k // EC, k % EC
                state = slice(c * STATES + g * GROUP, c * STATES + (g + 1) * GROUP)
                dve.wait_ge(inject_made, STEPS * u + k + 1)
                if h == 1:
                    dve.wait_ge(hlast_saved, STEPS * j + k + 1)
                for n in range(GROUP):
                    dve.wait_ge(decay_made, GROUP * (STEPS * u + k) + n + 1)
                    start = hlast[:, state.start + n:state.start + n + 1] if h else 0.0
                    i = dve.tensor_tensor_scan(hx[c][:, n, :], decay[k % 2][:, n, :], hx[c][:, n, :], start,
                                               ALU.mult, ALU.add)
                i.then_inc(scan_done, 1)
                dve.wait_ge(scan_done, STEPS * u + k + 1)
                if h == 0:
                    dve.tensor_copy(hlast[:, state], hx[c][:, :, TOK - 1]).then_inc(hlast_saved, 1)
                    dve.wait_ge(hlast_saved, STEPS * j + k + 1)
                dve.wait_ge(c_made, STATES * u + GROUP * (g + 1))
                dve.tensor_tensor(hx[c][:], hx[c][:], c_all[g % 2][:], ALU.mult).then_inc(hc_made, 1)

            def gate_output(w, h, c):
                dve.wait_ge(ysum_done, STEPS * w + (NG - 1) * EC + c + 1)
                dve.wait_ge(gate_made, NT * (w + 1))
                if past(EC * w + c - 1):
                    dve.wait_ge(back_full, EC * w + c - 1)
                dve.tensor_tensor(yg[c % 2][:], ysum[c][:].rearrange("p (t e) -> p t e", e=P),
                                  gate[h][:, :, c * P:(c + 1) * P], ALU.mult).then_inc(yg_made, 1)

            def add_residual(j, h):
                w = 2 * j + h
                dve.wait_ge(rc_loaded, 16 * (w + 1))
                for i in range(2):
                    dve.wait_ge(out_full, 2 * w + i + 1)
                    part = r_c[:, 2 * i:2 * i + 2, :]
                    dve.tensor_tensor(part, part, pp[i][:].rearrange("p (t d) -> p t d", d=DIM),
                                      ALU.add).then_inc(r_made, 1)

            def stage(j, h, first=False, last=False):
                u = 2 * j + h
                jv, hv = j + h, 1 - h
                for k in range(STEPS):
                    recur(j, h, k)
                    if k < 2 and not first:
                        gate_output(u - 1, 1 - h, k + 2)
                    if k == 3 and not first:
                        add_residual(j + h - 1, 1 - h)
                    if not last:
                        if k == 6:
                            convolve(jv, hv, 0)
                        if k == 7:
                            convolve(jv, hv, 1)
                        if k == 13:
                            softplus_rest(jv, hv)
                        if k == 14:
                            softplus_linear(jv, hv)
                            softplus_sum(jv, hv)
                    if k >= 14:
                        gate_output(u, h, k - 14)

            convolve(0, 0, 0)
            convolve(0, 0, 1)
            softplus_rest(0, 0)
            softplus_linear(0, 0)
            dve.wait_ge(ln_one_made, 1)
            softplus_sum(0, 0)
            stage(0, 0, first=True)
            stage(0, 1)
            with dve.Fori(1, ROUNDS - 1) as j:
                stage(j, 0)
                stage(j, 1)
            stage(ROUNDS - 1, 0)
            stage(ROUNDS - 1, 1, last=True)
            gate_output(2 * ROUNDS - 1, 1, 2)
            gate_output(2 * ROUNDS - 1, 1, 3)
            add_residual(ROUNDS - 1, 1)

        @block.gpsimd
        def _(pool):
            def normalise(j, h):
                v = 2 * j + h
                pool.wait_ge(sq_made, NT * (v + 1))
                if past(v):
                    pool.wait_ge(hn_made, v)
                pool.tensor_tensor(msq[:], sq[:], per_dim[:], ALU.mult).then_inc(rs_made, 1)
                pool.wait_ge(rs_made, 3 * v + 1)
                pool.tensor_tensor(msq[:], msq[:], eps[:], ALU.add).then_inc(rs_made, 1)
                pool.wait_ge(rs_made, 3 * v + 2)
                pool.tensor_tensor(rs[:], msq[:], neg_half[:], ALU.pow).then_inc(rs_made, 1)
                pool.wait_ge(rs_made, 3 * v + 3)
                pool.tensor_tensor(r_a[:], r_a[:], rs[:].rearrange("p (t a) -> p t a", a=1).to_broadcast([P, NT, DIM]),
                                   ALU.mult).then_inc(hn_made, 1)

            def lead(j, h):
                v = 2 * j + h
                if past(v):
                    pool.wait_ge(conv_done, EC * (TAPS - 1) * v)
                before = xi[:, :, TOK:TOK + TAPS - 1] if h == 1 else zeros[:]
                pool.tensor_tensor(xi[:, :, 0:TAPS - 1], before, zeros[:], ALU.add).then_inc(lead_made, 1)

            def make_dtu(v, h, c):
                pool.wait_ge(dt_made, v + 1)
                pool.wait_ge(u_made, v + 1)
                pool.tensor_tensor(dtu[h][:, c, :], dt[h][:, c, :], uu[:, c, :], ALU.mult).then_inc(dtu_made, 1)

            def inject(u, h, k):
                g, c = k // EC, k % EC
                if g == 0:
                    make_dtu(u, h, c)
                    pool.wait_ge(dtu_made, EC * u + c + 1)
                pool.wait_ge(b_made, STATES * u + GROUP * (g + 1))
                if past(STEPS * u + k - EC + 1):
                    pool.wait_ge(ysum_done, STEPS * u + k - EC + 1)
                pool.tensor_tensor(hx[c][:], dtu[h][:, c:c + 1, :].to_broadcast([P, GROUP, TOK]), b_all[g % 2][:],
                                   ALU.mult).then_inc(inject_made, 1)

            def stage(j, h, first=False, last=False):
                u = 2 * j + h
                jv, hv = j + h, 1 - h
                for k in range(STEPS):
                    inject(u, h, k)
                    if not last:
                        if k == 2:
                            normalise(jv, hv)
                        if k == 3:
                            lead(jv, hv)

            make_identity(pool, ident, ident_made)
            for tile, value in ((neg_half, -0.5), (eps, EPS), (per_dim, 1.0 / DIM), (zeros, 0.0)):
                pool.memset(tile[:], value).then_inc(ident_made, 1)
            pool.wait_ge(ident_made, 6)
            normalise(0, 0)
            lead(0, 0)
            stage(0, 0, first=True)
            stage(0, 1)
            with pool.Fori(1, ROUNDS - 1) as j:
                stage(j, 0)
                stage(j, 1)
            stage(ROUNDS - 1, 0)
            stage(ROUNDS - 1, 1, last=True)


def feed_forward(nc, x, residual, exact, norm_f, w1, w2, h1, h2, w3, scales, w3_scale, out):
    units = BATCH * HALVES
    LN_ATT, LN_IN, LN_OUT = range(3)
    GATE, UP, MID1, MID2 = range(4)
    with ExitStack() as ctx:
        def sb(name, shape):
            return ctx.enter_context(nc.sbuf_tensor(name, shape, F32))

        def psum(name):
            return ctx.enter_context(nc.psum_tensor(name, [P, TOK], F32))

        def sem(name):
            return ctx.enter_context(nc.semaphore(name))

        ident = sb("f_ident", [P, P])
        neg_half, eps, per_dim = sb("f_neg_half", [P, NT]), sb("f_eps", [P, NT]), sb("f_per_dim", [P, NT])
        spare = sb("f_spare", [P, 1])
        sc_sb = sb("sc_sb", [P, 4, HC])
        s3_sb = sb("s3_sb", [P, DIM])
        nf_sb = sb("nf_sb", [P, DIM])
        r_in = sb("f_r", [P, NT, DIM])
        x_in = sb("f_x", [P, NT, DIM])
        x1_next = sb("f_x1_next", [P, NT, DIM])
        x1 = sb("f_x1", [P, NT, DIM])
        y = sb("f_y", [P, NT, DIM])
        raw = [sb(f"f_raw{i}", [P, TOK]) for i in range(4)]

        def operands(split):
            n, dtype, kind = (2, F32R, "split") if split else (1, F32, "whole")
            with ExitStack() as place:
                def tile(name, shape):
                    return place.enter_context(nc.sbuf_tensor(f"f_{name}_{kind}", shape, dtype))

                weights = (tile("w1", [P, DC, HIDDEN]), tile("w2", [P, DC, HIDDEN]), tile("h1", [P, HC, HIDDEN]),
                           tile("h2", [P, HC, HIDDEN]), tile("w3", [P, HC, DIM]))
                yT, ha, hb = tile("yT", [P, n, DC, TOK]), tile("ha", [P, n, HC, TOK]), tile("hb", [P, n, HC, TOK])
            return weights, yT, (ha, hb, ha)

        exact_sb = ctx.enter_context(nc.sbuf_tensor("f_exact_sb", [1, 1], I32))
        o_sb = sb("f_o", [P, NT, DIM])
        sq = sb("f_sq", [P, NT])
        msq = sb("f_msq", [P, NT])
        rms = sb("f_rms", [P, NT])
        stats = [sb(f"f_stats{i}", [P, NT, 6]) for i in range(3)]
        mom = [sb(f"f_mom{i}", [P, NT, 2]) for i in range(3)]
        var = [sb(f"f_var{i}", [P, NT]) for i in range(3)]
        rstd = [sb(f"f_rstd{i}", [P, NT]) for i in range(3)]

        by_program = {split: operands(split) for split in (True, False)}

        pm = [psum(f"pm{i}") for i in range(4)]
        pt = [psum(f"pt{i}") for i in range(2)]
        po = [psum(f"po{i}") for i in range(2)]

        made = sem("f_made")
        w12_loaded, h1_loaded, h2_loaded, w3_loaded = (sem(f"f_{n}_loaded") for n in ("w12", "h1", "h2", "w3"))
        small_loaded = sem("f_small_loaded")
        r_loaded, x_loaded, out_stored = sem("f_r_loaded"), sem("f_x_loaded"), sem("f_out_stored")
        sq_made, msq_made, rms_made = sem("f_sq_made"), sem("f_msq_made"), sem("f_rms_made")
        stats_made = [sem(f"f_stats_made{i}") for i in range(3)]
        mom_made = [sem(f"f_mom_made{i}") for i in range(3)]
        var_made = [sem(f"f_var_made{i}") for i in range(3)]
        rstd_made = [sem(f"f_rstd_made{i}") for i in range(3)]
        att_scaled, att_normed, x1_made, y_made = (sem(f"f_{n}") for n in ("att_scaled", "att_normed", "x1_made", "y_made"))
        x1_moved = sem("f_x1_moved")
        yT_full, yT_made = sem("f_yT_full"), sem("f_yT_made")
        exact_loaded, yT_low_made = sem("f_exact_loaded"), sem("f_yT_low_made")
        gate_full, up_full, mid1_full, mid2_full = (sem(f"f_{n}_full") for n in ("gate", "up", "mid1", "mid2"))
        silu_made = sem("f_silu_made")
        chunk_made = [sem(f"f_chunk_made{i}") for i in range(3)]
        high_made = [sem(f"f_high_made{i}") for i in range(3)]
        low_made = [sem(f"f_low_made{i}") for i in range(3)]
        o_full, o_scaled, o_normed, o_made = (sem(f"f_{n}") for n in ("o_full", "o_scaled", "o_normed", "o_made"))

        block = ctx.enter_context(nc.Block())

        def parts(split):
            return range(2 if split else 1)

        def chunk(layer, o, split):
            hidden = by_program[split][2]
            return raw[o % 4][:] if split else hidden[layer][:, 0, o, :]

        def choose(engine, program):
            engine.wait_ge(exact_loaded, 16)
            flag = engine.value_load(exact_sb[0:1, 0:1])
            with engine.If(flag == 1):
                program(True)
            with engine.Else():
                program(False)

        def res_rows(u):
            seq = u // HALVES
            pair = seq // PAIR
            return rows((pair + 1) * (PER_PAIR + PAIR) - PAIR + seq % PAIR, u % HALVES)

        @block.sync
        def _(sp):
            def load(u):
                if past(u):
                    sp.wait_ge(x1_made, u)
                sp.dma_start(r_in[:], tokens_view(residual[res_rows(u), :])).then_inc(r_loaded, 16)
                sp.dma_start(x_in[:], tokens_view(x[bass.ds(u * TOK, TOK), :])).then_inc(x_loaded, 16)

            def store(u):
                sp.wait_ge(o_made, u + 1)
                sp.dma_start(tokens_view(out[bass.ds(u * TOK, TOK), :]), o_sb[:]).then_inc(out_stored, 16)

            sp.dma_start(exact_sb[:], exact).then_inc(exact_loaded, 16)
            load(0)
            load(1)
            with sp.Fori(0, units - 2) as u:
                load(u + 2)
                store(u)
            store(units - 2)
            store(units - 1)
            sp.wait_ge(out_stored, 16 * units)

        @block.tensor
        def _(pe):
            def transposes(u, split):
                pe.wait_ge(y_made, NT * (u + 1))
                if past(u):
                    pe.wait_ge(yT_made, DC * u)
                    if split:
                        pe.wait_ge(yT_low_made, DC * u)
                for c in range(DC):
                    for t in range(NT):
                        i = pe.transpose(pt[c][:, t * P:(t + 1) * P], y[:, t, c * P:(c + 1) * P], ident[:])
                    i.then_inc(yT_full, 1)

            def await_chunk(u, layer, k, split):
                if split:
                    pe.wait_ge(high_made[layer], HC * u + k + 1)
                    pe.wait_ge(low_made[layer], HC * u + k + 1)
                else:
                    pe.wait_ge(chunk_made[layer], HC * u + k + 1)

            def gated_layers(u, split):
                (w1_sb, w2_sb, *_), yT, _ = by_program[split]
                pe.wait_ge(yT_made, DC * (u + 1))
                if split:
                    pe.wait_ge(yT_low_made, DC * (u + 1))
                pe.wait_ge(w12_loaded, 32)
                for o in range(HC):
                    gate, up = pm[2 * o % 4], pm[(2 * o + 1) % 4]
                    if o >= 2:
                        pe.wait_ge(chunk_made[0], HC * u + o - 2 + 1)
                    elif past(u):
                        pe.wait_ge(chunk_made[2], HC * u)
                    for w_sb, tile, full in ((w1_sb, gate, gate_full), (w2_sb, up, up_full)):
                        for k in range(DC):
                            for part in parts(split):
                                i = pe.matmul(tile[:], w_sb[:, k, o * P:(o + 1) * P],
                                              yT[:, part, k, :], start=(k == 0 and part == 0),
                                              stop=(k == DC - 1 and part == parts(split)[-1]))
                        i.then_inc(full, 1)

            def middle_layer(u, w_sb, loaded, layer, full, split):
                hidden = by_program[split][2]
                before = layer - 1
                pe.wait_ge(loaded, 16)
                pe.wait_ge(chunk_made[before], HC * u + (7 if before == 0 else 5))
                for o in range(HC):
                    if o >= 4:
                        pe.wait_ge(chunk_made[layer], HC * u + o - 4 + 1)
                    for k in range(HC):
                        if o == 0:
                            await_chunk(u, before, k, split)
                        for part in parts(split):
                            i = pe.matmul(pm[o % 4][:], w_sb[:, k, o * P:(o + 1) * P],
                                          hidden[before][:, part, k, :],
                                          start=(k == 0 and part == 0),
                                          stop=(k == HC - 1 and part == parts(split)[-1]))
                    i.then_inc(full, 1)

            def last_layer(u, split):
                (*_, w3_sb), _, hidden = by_program[split]
                pe.wait_ge(w3_loaded, 16)
                if past(u):
                    pe.wait_ge(o_scaled, 2 * u)
                for half in range(2):
                    for t in range(2):
                        tok = (2 * half + t) * P
                        for k in range(HC):
                            if half == 0 and t == 0:
                                await_chunk(u, 2, k, split)
                            for part in parts(split):
                                i = pe.matmul(po[half][:, t * DIM:(t + 1) * DIM],
                                              hidden[2][:, part, k, tok:tok + P],
                                              w3_sb[:, k, :], start=(k == 0 and part == 0),
                                              stop=(k == HC - 1 and part == parts(split)[-1]))
                    i.then_inc(o_full, 1)

            def program(split):
                h1_sb, h2_sb = by_program[split][0][2:4]

                def unit(u, last=False):
                    gated_layers(u, split)
                    middle_layer(u, h1_sb, h1_loaded, 1, mid1_full, split)
                    middle_layer(u, h2_sb, h2_loaded, 2, mid2_full, split)
                    if not last:
                        transposes(u + 1, split)
                    last_layer(u, split)

                transposes(0, split)
                unit(0)
                with pe.Fori(1, units - 1) as u:
                    unit(u)
                unit(units - 1, last=True)

            pe.wait_ge(made, 2)
            choose(pe, program)

        @block.scalar
        def _(act):
            def squares(u):
                act.wait_ge(r_loaded, 16 * (u + 1))
                if past(u):
                    act.wait_ge(yT_full, DC * u)
                    act.wait_ge(msq_made, 2 * u)
                for t in range(NT):
                    act.activation(y[:, t, :], r_in[:, t, :], ACT.Square,
                                   accum_out=sq[:, t:t + 1]).then_inc(sq_made, 1)

            def take_yT(u, split):
                yT = by_program[split][1]
                if past(u):
                    act.wait_ge(up_full, HC * u)
                for c in range(DC):
                    act.wait_ge(yT_full, DC * u + c + 1)
                    act.activation(yT[:, 0, c, :], pt[c][:], ACT.Copy).then_inc(yT_made, 1)

            def await_raw(u, layer, o):
                if o >= 4:
                    act.wait_ge(low_made[layer], HC * u + o - 4 + 1)
                elif layer > 0:
                    act.wait_ge(low_made[layer - 1], HC * u + o + 4 + 1)
                elif past(u):
                    act.wait_ge(low_made[2], HC * (u - 1) + o + 4 + 1)

            def high(u, layer, o):
                hidden = by_program[True][2]
                act.wait_ge(chunk_made[layer], HC * u + o + 1)
                act.activation(hidden[layer][:, 0, o, :], raw[o % 4][:],
                               ACT.Copy).then_inc(high_made[layer], 1)

            def layer_outputs(u, layer, split):
                full = (gate_full, mid1_full, mid2_full)[layer]
                func = ACT.Silu if layer == 0 else ACT.Gelu
                scales = (GATE, MID1, MID2)[layer]
                for o in range(HC):
                    if split:
                        await_raw(u, layer, o)
                    act.wait_ge(full, HC * u + o + 1)
                    tile = pm[2 * o % 4] if layer == 0 else pm[o % 4]
                    act.activation(chunk(layer, o, split), tile[:], func, scale=sc_sb[:, scales, o:o + 1]).then_inc(
                        silu_made if layer == 0 else chunk_made[layer], 1)
                    if split and o >= 1:
                        high(u, layer, o - 1)
                if split:
                    high(u, layer, HC - 1)

            def program(split):
                def unit(u, last=False):
                    if past(u):
                        act.wait_ge(o_full, 2 * u)
                    layer_outputs(u, 0, split)
                    if not last:
                        squares(u + 1)
                    if past(u):
                        act.wait_ge(mid2_full, HC * u)
                    layer_outputs(u, 1, split)
                    act.wait_ge(mid1_full, HC * (u + 1))
                    layer_outputs(u, 2, split)
                    if not last:
                        take_yT(u + 1, split)

                take_yT(0, split)
                act.wait_ge(small_loaded, 48)
                unit(0)
                with act.Fori(1, units - 1) as u:
                    unit(u)
                unit(units - 1, last=True)

            act.dma_start(nf_sb[:], norm_f.rearrange("(a d) -> a d", a=1).to_broadcast([P, DIM])).then_inc(small_loaded, 16)
            act.dma_start(s3_sb[:], w3_scale.rearrange("(a d) -> a d", a=1).to_broadcast([P, DIM])).then_inc(small_loaded, 16)
            act.dma_start(sc_sb[:], scales).then_inc(small_loaded, 16)
            squares(0)
            choose(act, program)

        @block.vector
        def _(dve):
            def moments(u, which, src):
                for t in range(NT):
                    dve.bn_stats(stats[which][:, t, :], src[:, t, :]).then_inc(stats_made[which], 1)
                dve.wait_ge(stats_made[which], NT * (u + 1))
                dve.tensor_copy(spare[:], s3_sb[:, 0:1])
                for t in range(NT):
                    dve.bn_aggr(mom[which][:, t, :], stats[which][:, t, :]).then_inc(mom_made[which], 1)
                dve.wait_ge(mom_made[which], NT * (u + 1))
                dve.tensor_scalar(var[which][:], mom[which][:, :, 1], EPS, None, ALU.add).then_inc(var_made[which], 1)

            def normalise(u, which, src, dst, done):
                dve.wait_ge(rstd_made[which], u + 1)
                for t in range(NT):
                    dve.tensor_scalar(dst[:, t, :], src[:, t, :], mom[which][:, t, 0:1], rstd[which][:, t:t + 1],
                                      ALU.subtract, ALU.mult).then_inc(done, 1)

            def scale_att(u):
                dve.wait_ge(rms_made, u + 1)
                for t in range(NT):
                    dve.scalar_tensor_tensor(out=r_in[:, t, :], in0=r_in[:, t, :], scalar=rms[:, t:t + 1],
                                             in1=nf_sb[:], op0=ALU.mult, op1=ALU.mult).then_inc(att_scaled, 1)
                dve.wait_ge(att_scaled, NT * (u + 1))
                moments(u, LN_ATT, r_in)

            def make_x1(u):
                normalise(u, LN_ATT, r_in, r_in, att_normed)
                dve.wait_ge(att_normed, NT * (u + 1))
                dve.wait_ge(x_loaded, 16 * (u + 1))
                dve.tensor_tensor(x1_next[:], x_in[:], r_in[:], ALU.add).then_inc(x1_made, 1)
                dve.wait_ge(x1_made, u + 1)
                moments(u, LN_IN, x1_next)

            def make_y(u):
                normalise(u, LN_IN, x1_next, y, y_made)

            def yT_low(u):
                yT = by_program[True][1]
                for c in range(DC):
                    dve.wait_ge(yT_made, DC * u + c + 1)
                    dve.tensor_tensor(yT[:, 1, c, :], pt[c][:], yT[:, 0, c, :],
                                      ALU.subtract).then_inc(yT_low_made, 1)

            def low(u, layer, o):
                hidden = by_program[True][2]
                dve.wait_ge(high_made[layer], HC * u + o + 1)
                dve.tensor_tensor(hidden[layer][:, 1, o, :], raw[o % 4][:],
                                  hidden[layer][:, 0, o, :], ALU.subtract).then_inc(low_made[layer], 1)

            def gated(u, split):
                for o in range(HC):
                    dve.wait_ge(silu_made, HC * u + o + 1)
                    dve.wait_ge(up_full, HC * u + o + 1)
                    tile = chunk(0, o, split)
                    dve.scalar_tensor_tensor(out=tile, in0=pm[(2 * o + 1) % 4][:], scalar=sc_sb[:, UP, o:o + 1],
                                             in1=tile, op0=ALU.mult, op1=ALU.mult).then_inc(chunk_made[0], 1)
                    if split and o >= 1:
                        low(u, 0, o - 1)
                if split:
                    low(u, 0, HC - 1)

            def scale_out(u):
                if past(u):
                    dve.wait_ge(out_stored, 16 * u)
                for half in range(2):
                    dve.wait_ge(o_full, 2 * u + half + 1)
                    dve.tensor_tensor(o_sb[:, 2 * half:2 * half + 2, :],
                                      po[half][:].rearrange("p (t d) -> p t d", d=DIM),
                                      s3_sb[:].rearrange("p (a d) -> p a d", a=1).to_broadcast([P, 2, DIM]),
                                      ALU.mult).then_inc(o_scaled, 1)
                dve.wait_ge(o_scaled, 2 * (u + 1))
                moments(u, LN_OUT, o_sb)

            def add_out(u):
                normalise(u, LN_OUT, o_sb, o_sb, o_normed)
                dve.wait_ge(o_normed, NT * (u + 1))
                dve.tensor_tensor(o_sb[:], o_sb[:], x1[:], ALU.add).then_inc(o_made, 1)

            def move_x1(u):
                if past(u):
                    dve.wait_ge(o_made, u)
                dve.tensor_copy(x1[:], x1_next[:]).then_inc(x1_moved, 1)
                dve.wait_ge(x1_moved, u + 1)

            def program(split):
                def unit(u, first=False, last=False):
                    gated(u, split)
                    for o in range(HC):
                        if o == 0 and not first:
                            scale_out(u - 1)
                        if o == 1:
                            if not first:
                                add_out(u - 1)
                            move_x1(u)
                        if not last:
                            if o == 3:
                                scale_att(u + 1)
                            if o == 5:
                                make_x1(u + 1)
                            if o == 7:
                                make_y(u + 1)
                        if split:
                            low(u, 1, o)
                    if split:
                        for o in range(HC):
                            low(u, 2, o)
                        if not last:
                            yT_low(u + 1)

                if split:
                    yT_low(0)
                unit(0, first=True)
                with dve.Fori(1, units - 1) as u:
                    unit(u)
                unit(units - 1, last=True)

            dve.wait_ge(small_loaded, 48)
            scale_att(0)
            make_x1(0)
            make_y(0)
            choose(dve, program)
            scale_out(units - 1)
            add_out(units - 1)

        @block.gpsimd
        def _(pool):
            def load_weights(split):
                loads = zip((w1, w2, h1, h2, w3), by_program[split][0],
                            (w12_loaded, w12_loaded, h1_loaded, h2_loaded, w3_loaded))
                for dram, tile, loaded in loads:
                    pool.dma_start(tile[:], dram.rearrange("(c p) o -> p c o", p=P)).then_inc(loaded, 16)

            def root(u, which):
                pool.wait_ge(var_made[which], u + 1)
                pool.tensor_tensor(rstd[which][:], var[which][:], neg_half[:], ALU.pow).then_inc(rstd_made[which], 1)

            def root_mean_square(u):
                pool.wait_ge(sq_made, NT * (u + 1))
                if past(u):
                    pool.wait_ge(rms_made, u)
                    pool.wait_ge(att_scaled, NT * u)
                pool.tensor_tensor(msq[:], sq[:], per_dim[:], ALU.mult).then_inc(msq_made, 1)
                pool.wait_ge(msq_made, 2 * u + 1)
                pool.tensor_tensor(msq[:], msq[:], eps[:], ALU.add).then_inc(msq_made, 1)
                pool.wait_ge(msq_made, 2 * u + 2)
                pool.tensor_tensor(rms[:], msq[:], neg_half[:], ALU.pow).then_inc(rms_made, 1)

            def unit(u, first=False, last=False):
                if not first:
                    root(u - 1, LN_OUT)
                if not last:
                    root_mean_square(u + 1)
                    root(u + 1, LN_ATT)
                    root(u + 1, LN_IN)

            make_identity(pool, ident, made)
            for tile, value in ((neg_half, -0.5), (eps, EPS), (per_dim, 1.0 / DIM)):
                pool.memset(tile[:], value).then_inc(made, 1)
            choose(pool, load_weights)
            pool.wait_ge(made, 5)
            root_mean_square(0)
            root(0, LN_ATT)
            root(0, LN_IN)
            unit(0, first=True)
            with pool.Fori(1, units - 1) as u:
                unit(u)
            unit(units - 1, last=True)
            root(units - 1, LN_OUT)


def build(nc, x, w_in, w_x, w_dt, w_out, vectors, a_log, norm_f, w1, w2, h1, h2, w3, scales, w3_scale, out):
    residual = nc.dram_tensor("residual", [SLOTS * LENGTH, DIM], F32).ap()
    exact = nc.dram_tensor("exact", [1, 1], I32).ap()
    normalise_input(nc, x, residual, (w1, w2, h1, h2, w3), exact)
    mamba_layers(nc, residual, w_in, w_x, w_dt, w_out, vectors, a_log)
    feed_forward(nc, x, residual, exact, norm_f, w1, w2, h1, h2, w3, scales, w3_scale, out)


def by_partition(np, a):
    layers, channels = a.shape[:2]
    return a.reshape(layers, channels // P, P, -1).transpose(0, 2, 1, 3).reshape(layers, P, -1)


def kernel(**inputs):
    import numpy as np
    import concourse.bacc as bacc
    from concourse.bass_utils import run_bass_kernel_spmd

    a = {k.replace("L0_attn_", "").replace("L0_ffn_", ""): np.asarray(v) for k, v in inputs.items()}
    arrays = {
        "x": a["hidden_states"].reshape(BATCH * LENGTH, DIM),
        "w_in": a["in_proj_w"].transpose(0, 2, 1),
        "w_x": a["x_proj_w"].transpose(0, 2, 1),
        "w_dt": a["dt_proj_w"].transpose(0, 2, 1),
        "w_out": a["out_proj_w"].transpose(0, 2, 1),
        "vectors": np.concatenate([by_partition(np, a[k]) for k in
                                   ("norm_w", "conv_w", "conv_b", "dt_proj_b", "D_param")], axis=2),
        "a_log": by_partition(np, a["A_log"]),
        "norm_f": a["norm_f_w"],
        "w1": a["w1_w"].T, "w2": a["w2_w"].T, "h1": a["h1_w"].T, "h2": a["h2_w"].T, "w3": a["w3_w"].T,
        "scales": np.stack([a[k].reshape(HC, P).T for k in ("w1_s", "w2_s", "h1_s", "h2_s")], axis=1),
        "w3_scale": a["w3_s"],
    }
    arrays = {k: np.ascontiguousarray(v) for k, v in arrays.items()}
    nc = bacc.Bacc("TRN2", target_bir_lowering=False, num_devices=1)
    aps = {k: nc.dram_tensor(f"{k}_dram", v.shape, F32, kind="ExternalInput").ap() for k, v in arrays.items()}
    out = nc.dram_tensor("out_dram", (BATCH * LENGTH, DIM), F32, kind="ExternalOutput").ap()
    build(nc, out=out, **aps)
    r = run_bass_kernel_spmd(nc, [{f"{k}_dram": v for k, v in arrays.items()}], core_ids=[0])
    return r.results[0]["out_dram"].reshape(BATCH, LENGTH, DIM)
```
